# Optimizing a Trainium2 kernel written in Bass

```python
import numpy as np
import jax
import jax.numpy as jnp

def _softmax(x, axis=-1):
    return jax.nn.softmax(x, axis=axis)

def _gelu(x):
    return jax.nn.gelu(x, approximate=True)

def _silu(x):
    return jax.nn.silu(x)

def _sigmoid(x):
    return jax.nn.sigmoid(x)

def _layernorm(x, axis=-1, eps=1e-05):
    m = jnp.mean(x, axis=axis, keepdims=True)
    v = jnp.var(x, axis=axis, keepdims=True)
    return (x - m) / jnp.sqrt(v + eps)

def _scatter_add(tgt, idx, src, axis=0):
    return tgt.at[idx].add(src)

def _segment_sum(src, seg, n):
    return jax.ops.segment_sum(src, seg, n)
kernel_name = 'mk_rec_standalone_d1_rec_r8_f6aee1'

def setup_inputs(seed: int=0):
    np.random.seed(seed)
    _w = jnp.asarray

    def _rec_inputs():
        import jax
        import jax.numpy as jnp
        _rk = jax.random.key(seed)
        r_items = jnp.stack([jax.random.randint(jax.random.fold_in(jax.random.fold_in(_rk, 1), 0), (1024,), 106, 99921, jnp.int32), jax.random.randint(jax.random.fold_in(jax.random.fold_in(_rk, 1), 1), (1024,), 89, 99959, jnp.int32), jax.random.randint(jax.random.fold_in(jax.random.fold_in(_rk, 1), 2), (1024,), 2, 99940, jnp.int32), jax.random.randint(jax.random.fold_in(jax.random.fold_in(_rk, 1), 3), (1024,), 316, 99940, jnp.int32), jax.random.randint(jax.random.fold_in(jax.random.fold_in(_rk, 1), 4), (1024,), 297, 12448, jnp.int32), jax.random.randint(jax.random.fold_in(jax.random.fold_in(_rk, 1), 5), (1024,), 329, 99746, jnp.int32), jax.random.randint(jax.random.fold_in(jax.random.fold_in(_rk, 1), 6), (1024,), 114, 12470, jnp.int32), jax.random.randint(jax.random.fold_in(jax.random.fold_in(_rk, 1), 7), (1024,), 412, 99717, jnp.int32), jax.random.randint(jax.random.fold_in(jax.random.fold_in(_rk, 1), 8), (1024,), 92, 99874, jnp.int32), jax.random.randint(jax.random.fold_in(jax.random.fold_in(_rk, 1), 9), (1024,), 300, 99932, jnp.int32), jax.random.randint(jax.random.fold_in(jax.random.fold_in(_rk, 1), 10), (1024,), 24, 99983, jnp.int32), jax.random.randint(jax.random.fold_in(jax.random.fold_in(_rk, 1), 11), (1024,), 217, 99485, jnp.int32), jax.random.randint(jax.random.fold_in(jax.random.fold_in(_rk, 1), 12), (1024,), 96, 99965, jnp.int32), jax.random.randint(jax.random.fold_in(jax.random.fold_in(_rk, 1), 13), (1024,), 27, 99885, jnp.int32), jax.random.randint(jax.random.fold_in(jax.random.fold_in(_rk, 1), 14), (1024,), 333, 99890, jnp.int32), jax.random.randint(jax.random.fold_in(jax.random.fold_in(_rk, 1), 15), (1024,), 858, 99819, jnp.int32), jax.random.randint(jax.random.fold_in(jax.random.fold_in(_rk, 1), 16), (1024,), 104, 99919, jnp.int32), jax.random.randint(jax.random.fold_in(jax.random.fold_in(_rk, 1), 17), (1024,), 514, 99405, jnp.int32), jax.random.randint(jax.random.fold_in(jax.random.fold_in(_rk, 1), 18), (1024,), 173, 99881, jnp.int32), jax.random.randint(jax.random.fold_in(jax.random.fold_in(_rk, 1), 19), (1024,), 68, 99870, jnp.int32), jax.random.randint(jax.random.fold_in(jax.random.fold_in(_rk, 1), 20), (1024,), 58, 12490, jnp.int32), jax.random.randint(jax.random.fold_in(jax.random.fold_in(_rk, 1), 21), (1024,), 25, 99874, jnp.int32), jax.random.randint(jax.random.fold_in(jax.random.fold_in(_rk, 1), 22), (1024,), 14, 99834, jnp.int32), jax.random.randint(jax.random.fold_in(jax.random.fold_in(_rk, 1), 23), (1024,), 97, 99829, jnp.int32), jax.random.randint(jax.random.fold_in(jax.random.fold_in(_rk, 1), 24), (1024,), 185, 99827, jnp.int32), jax.random.randint(jax.random.fold_in(jax.random.fold_in(_rk, 1), 25), (1024,), 142, 99974, jnp.int32), jax.random.randint(jax.random.fold_in(jax.random.fold_in(_rk, 1), 26), (1024,), 64, 12462, jnp.int32), jax.random.randint(jax.random.fold_in(jax.random.fold_in(_rk, 1), 27), (1024,), 32, 99836, jnp.int32), jax.random.randint(jax.random.fold_in(jax.random.fold_in(_rk, 1), 28), (1024,), 89, 99501, jnp.int32), jax.random.randint(jax.random.fold_in(jax.random.fold_in(_rk, 1), 29), (1024,), 39, 99994, jnp.int32), jax.random.randint(jax.random.fold_in(jax.random.fold_in(_rk, 1), 30), (1024,), 256, 99911, jnp.int32), jax.random.randint(jax.random.fold_in(jax.random.fold_in(_rk, 1), 31), (1024,), 207, 99940, jnp.int32), jax.random.randint(jax.random.fold_in(jax.random.fold_in(_rk, 1), 32), (1024,), 15, 99969, jnp.int32), jax.random.randint(jax.random.fold_in(jax.random.fold_in(_rk, 1), 33), (1024,), 956, 12463, jnp.int32), jax.random.randint(jax.random.fold_in(jax.random.fold_in(_rk, 1), 34), (1024,), 360, 12429, jnp.int32), jax.random.randint(jax.random.fold_in(jax.random.fold_in(_rk, 1), 35), (1024,), 48, 99165, jnp.int32), jax.random.randint(jax.random.fold_in(jax.random.fold_in(_rk, 1), 36), (1024,), 85, 99979, jnp.int32), jax.random.randint(jax.random.fold_in(jax.random.fold_in(_rk, 1), 37), (1024,), 796, 12454, jnp.int32), jax.random.randint(jax.random.fold_in(jax.random.fold_in(_rk, 1), 38), (1024,), 37, 99778, jnp.int32), jax.random.randint(jax.random.fold_in(jax.random.fold_in(_rk, 1), 39), (1024,), 163, 99470, jnp.int32), jax.random.randint(jax.random.fold_in(jax.random.fold_in(_rk, 1), 40), (1024,), 36, 99913, jnp.int32), jax.random.randint(jax.random.fold_in(jax.random.fold_in(_rk, 1), 41), (1024,), 81, 99796, jnp.int32), jax.random.randint(jax.random.fold_in(jax.random.fold_in(_rk, 1), 42), (1024,), 37, 99549, jnp.int32), jax.random.randint(jax.random.fold_in(jax.random.fold_in(_rk, 1), 43), (1024,), 18, 99979, jnp.int32), jax.random.randint(jax.random.fold_in(jax.random.fold_in(_rk, 1), 44), (1024,), 433, 99883, jnp.int32), jax.random.randint(jax.random.fold_in(jax.random.fold_in(_rk, 1), 45), (1024,), 199, 12498, jnp.int32), jax.random.randint(jax.random.fold_in(jax.random.fold_in(_rk, 1), 46), (1024,), 67, 99691, jnp.int32), jax.random.randint(jax.random.fold_in(jax.random.fold_in(_rk, 1), 47), (1024,), 237, 99626, jnp.int32), jax.random.randint(jax.random.fold_in(jax.random.fold_in(_rk, 1), 48), (1024,), 471, 99786, jnp.int32), jax.random.randint(jax.random.fold_in(jax.random.fold_in(_rk, 1), 49), (1024,), 60, 99900, jnp.int32)], axis=1)
        r_inputs = jnp.stack([jax.random.randint(jax.random.fold_in(jax.random.fold_in(_rk, 2), 0), (1024,), 49, 12494, jnp.int32), jax.random.randint(jax.random.fold_in(jax.random.fold_in(_rk, 2), 1), (1024,), 171, 99937, jnp.int32), jax.random.randint(jax.random.fold_in(jax.random.fold_in(_rk, 2), 2), (1024,), 51, 99789, jnp.int32), jax.random.randint(jax.random.fold_in(jax.random.fold_in(_rk, 2), 3), (1024,), 91, 99950, jnp.int32), jax.random.randint(jax.random.fold_in(jax.random.fold_in(_rk, 2), 4), (1024,), 19, 99927, jnp.int32), jax.random.randint(jax.random.fold_in(jax.random.fold_in(_rk, 2), 5), (1024,), 306, 99709, jnp.int32), jax.random.randint(jax.random.fold_in(jax.random.fold_in(_rk, 2), 6), (1024,), 183, 99941, jnp.int32), jax.random.randint(jax.random.fold_in(jax.random.fold_in(_rk, 2), 7), (1024,), 277, 99862, jnp.int32), jax.random.randint(jax.random.fold_in(jax.random.fold_in(_rk, 2), 8), (1024,), 1, 99886, jnp.int32), jax.random.randint(jax.random.fold_in(jax.random.fold_in(_rk, 2), 9), (1024,), 179, 99173, jnp.int32), jax.random.randint(jax.random.fold_in(jax.random.fold_in(_rk, 2), 10), (1024,), 206, 99930, jnp.int32), jax.random.randint(jax.random.fold_in(jax.random.fold_in(_rk, 2), 11), (1024,), 57, 99945, jnp.int32), jax.random.randint(jax.random.fold_in(jax.random.fold_in(_rk, 2), 12), (1024,), 7, 99593, jnp.int32), jax.random.randint(jax.random.fold_in(jax.random.fold_in(_rk, 2), 13), (1024,), 9, 99854, jnp.int32), jax.random.randint(jax.random.fold_in(jax.random.fold_in(_rk, 2), 14), (1024,), 51, 99906, jnp.int32), jax.random.randint(jax.random.fold_in(jax.random.fold_in(_rk, 2), 15), (1024,), 769, 99243, jnp.int32), jax.random.randint(jax.random.fold_in(jax.random.fold_in(_rk, 2), 16), (1024,), 192, 99799, jnp.int32), jax.random.randint(jax.random.fold_in(jax.random.fold_in(_rk, 2), 17), (1024,), 249, 12468, jnp.int32), jax.random.randint(jax.random.fold_in(jax.random.fold_in(_rk, 2), 18), (1024,), 154, 99961, jnp.int32), jax.random.randint(jax.random.fold_in(jax.random.fold_in(_rk, 2), 19), (1024,), 58, 12489, jnp.int32), jax.random.randint(jax.random.fold_in(jax.random.fold_in(_rk, 2), 20), (1024,), 213, 99457, jnp.int32), jax.random.randint(jax.random.fold_in(jax.random.fold_in(_rk, 2), 21), (1024,), 290, 99972, jnp.int32), jax.random.randint(jax.random.fold_in(jax.random.fold_in(_rk, 2), 22), (1024,), 130, 99748, jnp.int32), jax.random.randint(jax.random.fold_in(jax.random.fold_in(_rk, 2), 23), (1024,), 197, 12485, jnp.int32), jax.random.randint(jax.random.fold_in(jax.random.fold_in(_rk, 2), 24), (1024,), 74, 99939, jnp.int32), jax.random.randint(jax.random.fold_in(jax.random.fold_in(_rk, 2), 25), (1024,), 101, 99988, jnp.int32), jax.random.randint(jax.random.fold_in(jax.random.fold_in(_rk, 2), 26), (1024,), 228, 99559, jnp.int32), jax.random.randint(jax.random.fold_in(jax.random.fold_in(_rk, 2), 27), (1024,), 532, 99886, jnp.int32), jax.random.randint(jax.random.fold_in(jax.random.fold_in(_rk, 2), 28), (1024,), 208, 99692, jnp.int32), jax.random.randint(jax.random.fold_in(jax.random.fold_in(_rk, 2), 29), (1024,), 255, 99932, jnp.int32), jax.random.randint(jax.random.fold_in(jax.random.fold_in(_rk, 2), 30), (1024,), 9, 99850, jnp.int32), jax.random.randint(jax.random.fold_in(jax.random.fold_in(_rk, 2), 31), (1024,), 454, 99977, jnp.int32), jax.random.randint(jax.random.fold_in(jax.random.fold_in(_rk, 2), 32), (1024,), 73, 99922, jnp.int32), jax.random.randint(jax.random.fold_in(jax.random.fold_in(_rk, 2), 33), (1024,), 258, 12477, jnp.int32), jax.random.randint(jax.random.fold_in(jax.random.fold_in(_rk, 2), 34), (1024,), 27, 99494, jnp.int32), jax.random.randint(jax.random.fold_in(jax.random.fold_in(_rk, 2), 35), (1024,), 164, 99406, jnp.int32), jax.random.randint(jax.random.fold_in(jax.random.fold_in(_rk, 2), 36), (1024,), 13, 99883, jnp.int32), jax.random.randint(jax.random.fold_in(jax.random.fold_in(_rk, 2), 37), (1024,), 109, 99773, jnp.int32), jax.random.randint(jax.random.fold_in(jax.random.fold_in(_rk, 2), 38), (1024,), 70, 99563, jnp.int32), jax.random.randint(jax.random.fold_in(jax.random.fold_in(_rk, 2), 39), (1024,), 136, 99982, jnp.int32), jax.random.randint(jax.random.fold_in(jax.random.fold_in(_rk, 2), 40), (1024,), 39, 99997, jnp.int32), jax.random.randint(jax.random.fold_in(jax.random.fold_in(_rk, 2), 41), (1024,), 243, 99948, jnp.int32), jax.random.randint(jax.random.fold_in(jax.random.fold_in(_rk, 2), 42), (1024,), 167, 99275, jnp.int32), jax.random.randint(jax.random.fold_in(jax.random.fold_in(_rk, 2), 43), (1024,), 387, 99981, jnp.int32), jax.random.randint(jax.random.fold_in(jax.random.fold_in(_rk, 2), 44), (1024,), 193, 99949, jnp.int32), jax.random.randint(jax.random.fold_in(jax.random.fold_in(_rk, 2), 45), (1024,), 12, 99422, jnp.int32), jax.random.randint(jax.random.fold_in(jax.random.fold_in(_rk, 2), 46), (1024,), 38, 99941, jnp.int32), jax.random.randint(jax.random.fold_in(jax.random.fold_in(_rk, 2), 47), (1024,), 27, 99546, jnp.int32), jax.random.randint(jax.random.fold_in(jax.random.fold_in(_rk, 2), 48), (1024,), 63, 99676, jnp.int32), jax.random.randint(jax.random.fold_in(jax.random.fold_in(_rk, 2), 49), (1024,), 1149, 99721, jnp.int32)], axis=1)
        r_alias_inputs = jax.random.randint(jax.random.fold_in(_rk, 3), (1024, 50), 0, 50, jnp.int32)
        return (r_items, r_inputs, r_alias_inputs)
    r_items, r_inputs, r_alias_inputs = _rec_inputs()

    def _L0_rec_setup():
        import jax, jax.numpy as jnp
        import numpy as np
        NUM_NODE = 12500
        DIM = 128
        B = 512
        L = 50
        LAYERS = 2
        N_EDGES = 150000
        W_K = 12.0
        EPS = 1e-12

        def _l2norm(x):
            n = jnp.linalg.norm(x, axis=-1, keepdims=True)
            return x / jnp.maximum(n, EPS)
        key = jax.random.key(seed)
        ks = jax.random.split(key, 13)
        N = NUM_NODE + 1
        items = jax.random.randint(ks[0], (B, L), 0, N)
        inputs = jax.random.randint(ks[1], (B, L), 0, N)
        alias_inputs = jax.random.randint(ks[2], (B, L), 0, L)
        item_features = jax.random.normal(ks[3], (N, DIM), jnp.float32) * 0.02
        adj_row = jax.random.randint(ks[4], (N_EDGES,), 0, N)
        adj_col = jax.random.randint(ks[5], (N_EDGES,), 0, N)
        adj_val = jax.random.uniform(ks[6], (N_EDGES,), jnp.float32)
        stdv = 1.0 / np.sqrt(DIM)
        u = lambda k, s: jax.random.uniform(k, s, jnp.float32, -stdv, stdv)
        emb = u(ks[7], (N, DIM)).at[0].set(0.0)
        w_1 = u(ks[8], (2 * DIM, DIM))
        w_2 = u(ks[9], (DIM, 1))
        glu1_w = u(ks[10], (DIM, DIM))
        glu1_b = u(ks[11], (DIM,))
        glu2_w = u(ks[12], (DIM, DIM))
        return {'items': items, 'inputs': inputs, 'alias_inputs': alias_inputs, 'item_features': item_features, 'adj_row': adj_row, 'adj_col': adj_col, 'adj_val': adj_val, 'emb': emb, 'w_1': w_1, 'w_2': w_2, 'glu1_w': glu1_w, 'glu1_b': glu1_b, 'glu2_w': glu2_w}
    _L0_rec_all = _L0_rec_setup()
    _L0_rec_in = {k: v for k, v in _L0_rec_all.items() if k in ('item_features', 'adj_row', 'adj_col', 'adj_val', 'emb', 'w_1', 'w_2', 'glu1_w', 'glu1_b', 'glu2_w')}
    del _L0_rec_all
    return {'r_items': r_items, 'r_inputs': r_inputs, 'r_alias_inputs': r_alias_inputs, 'L0_rec_item_features': _L0_rec_in['item_features'], 'L0_rec_adj_row': _L0_rec_in['adj_row'], 'L0_rec_adj_col': _L0_rec_in['adj_col'], 'L0_rec_adj_val': _L0_rec_in['adj_val'], 'L0_rec_emb': _L0_rec_in['emb'], 'L0_rec_w_1': _L0_rec_in['w_1'], 'L0_rec_w_2': _L0_rec_in['w_2'], 'L0_rec_glu1_w': _L0_rec_in['glu1_w'], 'L0_rec_glu1_b': _L0_rec_in['glu1_b'], 'L0_rec_glu2_w': _L0_rec_in['glu2_w']}

def reference(r_items, r_inputs, r_alias_inputs, L0_rec_item_features, L0_rec_adj_row, L0_rec_adj_col, L0_rec_adj_val, L0_rec_emb, L0_rec_w_1, L0_rec_w_2, L0_rec_glu1_w, L0_rec_glu1_b, L0_rec_glu2_w):
    import jax
    import jax.numpy as jnp

    def _L0_rec_ref(items, inputs, alias_inputs, item_features, adj_row, adj_col, adj_val, emb, w_1, w_2, glu1_w, glu1_b, glu2_w):
        import jax, jax.numpy as jnp
        import numpy as np
        NUM_NODE = 12500
        DIM = 128
        B = 512
        L = 50
        LAYERS = 2
        N_EDGES = 150000
        W_K = 12.0
        EPS = 1e-12

        def _l2norm(x):
            n = jnp.linalg.norm(x, axis=-1, keepdims=True)
            return x / jnp.maximum(n, EPS)
        N = emb.shape[0]
        h = emb
        acc = emb
        for _ in range(LAYERS):
            h = jax.ops.segment_sum(adj_val[:, None] * h[adj_col], adj_row, num_segments=N)
            acc = acc + h
        graph_item_embs = acc / (LAYERS + 1)
        combined = graph_item_embs[items] + item_features[items]
        seq_hidden = jnp.take_along_axis(combined, alias_inputs[..., None], axis=1)
        mask = (inputs != 0)[..., None].astype(seq_hidden.dtype)
        hs = jnp.sum(seq_hidden * mask, axis=1) / jnp.sum(mask, axis=1)
        pos_emb = jnp.flip(emb[:L], axis=0)
        pos_b = jnp.broadcast_to(pos_emb[None], seq_hidden.shape)
        nh = jnp.tanh(jnp.concatenate([pos_b, seq_hidden], axis=-1) @ w_1)
        nh = jax.nn.sigmoid(nh @ glu1_w.T + glu1_b + (hs @ glu2_w.T)[:, None, :])
        beta = nh @ w_2 * mask
        sess_emb = jnp.sum(beta * seq_hidden, axis=1)
        select = W_K * _l2norm(sess_emb)
        scores = select @ _l2norm(graph_item_embs).T
        return scores
    y = _L0_rec_ref(r_items, r_inputs, r_alias_inputs, L0_rec_item_features, L0_rec_adj_row, L0_rec_adj_col, L0_rec_adj_val, L0_rec_emb, L0_rec_w_1, L0_rec_w_2, L0_rec_glu1_w, L0_rec_glu1_b, L0_rec_glu2_w)
    return y

_drawn_inputs = setup_inputs


def setup_inputs(seed=0):
    import zlib

    import numpy as np

    out = dict(_drawn_inputs(seed))
    spreads = {}
    factors = {'L0_rec_w_1': 3.829, 'L0_rec_glu1_w': 3.834, 'L0_rec_glu1_b': 28.17, 'L0_rec_glu2_w': 8.0}
    for name, (base, spread) in spreads.items():
        noise = np.random.default_rng([zlib.crc32(name.encode()), seed]).standard_normal(out[name].shape)
        drawn = base * np.exp(spread * noise) if base else spread * noise
        out[name] = jnp.asarray(drawn.astype(out[name].dtype))
    for name, factor in factors.items():
        out[name] = (out[name] * factor).astype(out[name].dtype)
    return out
```

```python
from contextlib import ExitStack

import numpy as np

import concourse.bass as bass
from concourse import mybir

F32 = mybir.dt.float32
BF16 = mybir.dt.bfloat16
F16 = mybir.dt.float16
I32 = mybir.dt.int32
ALU = mybir.AluOpType
ACT = mybir.ActivationFunctionType
AX = mybir.AxisListType

P = 128
N, D = 12501, 128
E = 150000
EP = 125
EC = E // EP
R = 256
NB = -(-N // R)
NBLK = NB * R // P
FULL, LAST = N // P, N % P
GS = 8
SUB = 10
SC = GS * SUB
CHUNKS = [80, 160, 320, 320, 320]
assert sum(CHUNKS) == EC
W = 4
RING = 4
PW = 5
ROUND = W * RING
PTURN = PW * RING
CAPS = [-(-((EP * c + NB * (P - 1)) // P) // ROUND) * ROUND for c in CHUNKS]
CMAX, CAPMAX = max(CHUNKS), max(CAPS)
TILES = sum(CAPS)
TPAD = TILES + ROUND
TILE0 = [sum(CAPS[:k]) for k in range(len(CAPS) + 1)]
COL0 = [sum(CHUNKS[:k]) for k in range(len(CHUNKS) + 1)]
K = len(CHUNKS)
MID = CAPMAX // 2
LO = 11
COLBITS = 14
QT = -(-CAPMAX // P)
B, L = 1024, 50
ST = B // P
OBW = 512
OB = -(-N // OBW)
OG = 5
SG = 4
SGS = [(l, min(SG, L - l)) for l in range(0, L, SG)]
NG = len(SGS)
GL = 10
PIECES = 7
TR = NBLK // SG
W_K, EPS = 12.0, 1e-12
assert OB == 5 * OG and NBLK % PIECES == 0 and ST % 2 == 0


def sub_units(n):
    return n // SC


def build(nc, x, out):
    ctx = ExitStack()
    with ctx:
        def sb(name, shape, dt):
            return ctx.enter_context(nc.sbuf_tensor(name, shape, dt))

        def sem(name):
            return ctx.enter_context(nc.semaphore(name))

        WORDS = 48640
        arena = sb("arena", [P, WORDS], F32)
        top = [0]

        def view(words, shape, dt, at=None, parts=P):
            start = top[0] if at is None else at
            if at is None:
                top[0] += words
            assert start + words <= WORDS, (start, words)
            v = arena[0:parts, start:start + words]
            if dt is not F32:
                v = v.bitcast(dt)
            names = " ".join("abcd"[:len(shape)])
            sizes = {"abcd"[n]: s for n, s in enumerate(shape)}
            if len(shape) > 1:
                v = v.rearrange(f"p ({names}) -> p {names}", **sizes)
            return v

        ACCW = NBLK * D
        acc = view(ACCW, [ACCW], F32)[:, 0:NBLK * D]
        low = top[0]
        rows = view(EC, [EC], I32)
        cols = view(EC, [EC], I32)
        vals = view(EC, [EC], F32)
        lo, hi, v1, v2, v3, qf, tf, t0, t1, pk = (view(CMAX, [CMAX], F32 if n < 7 else I32) for n in range(10))
        r1 = view(CMAX, [CMAX], F32)
        binb = view(CMAX // 2, [CMAX], BF16)
        vb = view(CMAX // 2, [CMAX], BF16)
        oh = view(CMAX * NB // 2, [CMAX, NB], BF16)
        GMAX = CMAX // GS
        before = view(SC * NB // 2, [SUB, GS, NB], BF16)
        cnt_w = NB * GMAX
        cnt_at = top[0]
        top[0] += cnt_w
        inc_at = top[0]
        top[0] += cnt_w
        picked = view(2 * GS * NB, [2, GS, NB], F32)
        rst_at = top[0]
        oht = view(2 * PW * CAPMAX // 2, [2, PW, CAPMAX], BF16)
        ohq = view(2 * PW * P // 2, [2, PW, P], BF16)
        ohi = view(2 * PW * 2 * P // 2, [2, PW, 2 * P], F16)
        ohv = view(2 * PW * 3 * P // 2, [2, PW, 3 * P], BF16)
        high = top[0]
        idx_s = view(TPAD, [TPAD], I32)
        row_s = view(TPAD, [TPAD], F32)
        val_s = view(TPAD, [TPAD], F32)
        gath = view(RING * W * D, [RING, W, D], F32)
        hot = view(2 * W * R, [2, W, R], F32)

        total = view(ACCW, [ACCW], F32, at=low)
        seq = [view(L * D, [L, D], F32, at=a) for a in (0, low + ACCW)]
        stage = view(2 * OG * OBW, [2, OG * OBW], F32, at=L * D)
        nh_at = low + ACCW + L * D
        nh = view(L * P, [L * P], F32, at=nh_at)
        items_i, alias_i, inputs_i = (view(ST * L, [ST, L], I32, at=nh_at + n * ST * L) for n in range(3))
        wrap = view(ST * L, [ST, L], F32, at=nh_at + 3 * ST * L)
        top[0] = nh_at + L * P
        items_f = view(ST * L, [ST, L], F32)
        alias_f = view(ST * L, [ST, L], F32)
        mask = view(ST * L, [ST, L], F32)
        idx_f = view((ST + 1) * L, [ST + 1, L], F32)
        scrap = view(ST * L, [ST, L], F32)
        assert top[0] <= high
        top[0] = high
        seq_t = view(2 * SG * P, [2, SG * P], F32)
        gate = view(2 * SG * P, [2, SG * P], F32)
        turn_in = view(2 * SG * P, [2, SG, P], F32)
        square = view(D, [D], F32)
        hs = view(D, [D], F32)
        hs_n = view(D, [D], F32)
        hs_t = view(P, [P], F32)
        sess = view(D, [D], F32)
        sess_t = view(2 * P, [2, P], F32)
        sess_sq = view(D, [D], F32)
        beta = view(L, [L], F32)

        tiles_i = sb("tiles_i", [P, NB], I32)
        tiles_f = sb("tiles_f", [P, NB], F32)
        tiles_inc = sb("tiles_inc", [P, NB], F32)
        base = sb("base", [P, NB], F32)
        past = sb("past", [P, QT, NB - 1], F32)
        bin_of = sb("bin_of", [P, QT], F32)
        tab = sb("tab", [1, TPAD], I32)
        iring = sb("iring", [P, RING * W], I32)
        idx50 = sb("idx50", [P, 2, L], I32)
        w1a, w1b, g1, g2, g1_t, g2_t = (sb(n, [P, P], F32) for n in ("w1a", "w1b", "g1", "g2", "g1_t", "g2_t"))
        w2, gb = sb("w2", [P, 1], F32), sb("gb", [P, 1], F32)
        pos = sb("pos", [L, D], F32)
        pos_t = sb("pos_t", [D, L], F32)
        pos_w = sb("pos_w", [D, L], F32)
        n_in, cinv = sb("n_in", [P, ST], F32), sb("cinv", [P, ST], F32)
        row_ss, row_n = sb("row_ss", [P, NBLK], F32), sb("row_n", [P, NBLK], F32)
        ss, root, rsc = sb("ss", [P, 2], F32), sb("root", [P, 2], F32), sb("rsc", [P, 2], F32)
        iota_bin = sb("iota_bin", [P, NB], BF16)
        iota_q = sb("iota_q", [P, P], BF16)
        iota_t = sb("iota_t", [P, CAPMAX], BF16)
        iota_r = sb("iota_r", [P, R], F32)
        iota_tq = sb("iota_tq", [P, QT], F32)
        ident = sb("ident", [P, P], F32)
        below = sb("below", [P, P], BF16)
        ones_b = sb("ones_b", [P, P], BF16)
        zero_b = sb("zero_b", [P, P], BF16)
        ones_f = sb("ones_f", [P, P], F32)

        def bank(name):
            return ctx.enter_context(nc.psum_tensor(name, [P, 512], F32))

        ps_idx, ps_val = bank("ps_idx"), bank("ps_val")
        ps_rank = [bank("ps_rank0"), bank("ps_rank1")]
        ps_app = [ctx.enter_context(nc.psum_tensor(f"ps_app{n}", [P, W, R], F32)) for n in range(2)]

        s_rows, s_cols, s_vals = sem("rows_in"), sem("cols_in"), sem("vals_in")
        s_const = sem("constants_made")
        s_cz = sem("constants_cleared")
        s_dve = sem("vector_step")
        s_oh = sem("bins_onehot")
        s_ct = sem("group_counts")
        s_ctc = sem("group_counts_copied")
        s_cum = sem("prefix_counts")
        s_binof = sem("bin_of_tile")
        s_row1 = sem("bin_row_turned")
        s_tab = sem("bin_table_stored")
        s_before = sem("before_in_group")
        s_rank = sem("ranks_summed")
        s_pick = sem("ranks_picked")
        s_pd = sem("perm_onehots")
        s_pa = sem("perm_values")
        s_pm = sem("perm_matmuls")
        s_pz = sem("perm_banks_done")
        s_ev = sem("perm_banks_read")
        s_idx = sem("indices_in_ring")
        s_g = [sem(f"gathered{n}") for n in range(RING)]
        s_hot = sem("rows_onehot")
        s_mm = sem("tile_products")
        s_add = sem("halves_added")
        s_acc = sem("tiles_added")
        s_clear = sem("accumulator_clear")
        s_h1 = sem("layer1_done")
        s_h1w = sem("layer1_stored")
        s_emb = sem("embeddings_in")
        s_out = [sem(f"out_stored{n}") for n in range(2)]
        s_w, s_w2 = sem("weights_in"), sem("weights2_in")
        s_wt, s_wtc = sem("weights_turned"), sem("weights_copied")
        s_sorted = sem("edges_sorted")
        s_ids = sem("session_ids_in")
        s_total = sem("total_begun")
        s_feat = sem("features_in")
        s_comb = sem("combined_made")
        s_combw = sem("combined_stored")
        s_sel = sem("indices_selected")
        s_rss = sem("row_squares")
        s_rroot = sem("row_roots")
        s_scaled = sem("rows_scaled")
        s_turned = sem("rows_turned")
        s_norm = sem("rows_placed")
        s_sidx = sem("session_indices")
        s_seq = [[sem(f"seq{n}_{q}") for q in range(L // GL)] for n in range(2)]
        s_tr = sem("places_turned")
        s_seqt = sem("places_copied")
        s_m1 = sem("hidden_products")
        s_psm = sem("hidden_read")
        s_hsn = sem("mean_made")
        s_ht = sem("mean_turned")
        s_htc = sem("mean_copied")
        s_z = sem("gate_products")
        s_bt = sem("gates_summed")
        s_sess = sem("session_made")
        s_sst = sem("session_turned")
        s_sstc = sem("session_copied")
        s_ss = sem("session_square")
        s_root = sem("session_root")
        s_rsc = sem("session_scale")
        s_sc = [sem(f"score_block{n}") for n in range(2)]
        s_scev = [sem(f"score_staged{n}") for n in range(2)]
        s_free = sem("stage_free")
        s_staged = sem("stage_full")

        h1 = nc.dram_tensor("h1_rows", [NBLK * P, D], F32, kind="Internal").ap()
        comb = nc.dram_tensor("combined_rows", [NBLK * P, D], F32, kind="Internal").ap()
        ps_turn = [ps_idx, ps_val]
        ps_hid = ps_rank
        ps_beta = ps_app[0][:, 0, 0:L]
        ps_mean, ps_sess = ps_app[0][:, 2, 0:P], ps_app[0][:, 2, P:2 * P]
        ps_score = [ps_app[1][:, 2 * n:2 * n + 2, :].rearrange("p a b -> p (a b)") for n in range(2)]

        def wait(eng, s, value):
            if not isinstance(value, int) or value > 0:
                eng.wait_ge(s, value)

        def session_steps(eng, step):
            step(0, 0, None)
            with eng.Fori(0, (ST - 2) // 2) as i:
                step(2 * i + 1, 1, (i, 0))
                step(2 * i + 2, 0, (i, 1))
            step(ST - 1, 1, ((ST - 2) // 2, 0))

        LASTC = ((ST - 1) // 2, 1)

        def score_block(c, j):
            i, par = c
            n = OB * par + j
            return n % 2, OB * i + n // 2 + 1, j * OBW, min(OBW, N - j * OBW)

        def evacuate_scores(eng, mine, c, j):
            i, par = c
            b, n, at, w = score_block(c, j)
            if b != mine:
                return
            q, m = j // OG, OG * par + j // OG
            eng.wait_ge(s_sc[b], n)
            eng.wait_ge(s_rsc, 2 * i + par + 1)
            eng.wait_ge(s_free, 2 * OG * i + m + 1)
            dst = stage[:, m % 2, (j % OG) * OBW:(j % OG) * OBW + w]
            scale = rsc[:, par:par + 1]
            if mine:
                ins = eng.activation(dst, ps_score[b][:, 0:w], ACT.Copy, scale=scale)
            else:
                ins = eng.tensor_scalar(dst, ps_score[b][:, 0:w], scale, None, ALU.mult)
            ins.then_inc(s_scev[b], 1)

        halves = [c // W for c in CAPS]
        units = [c // PW for c in CHUNKS]
        phases = halves + [TILES // W]
        idx_base = [sum(phases[:n]) + RING * n for n in range(K + 2)]
        hot_base = [sum(phases[:n]) + 2 * n for n in range(K + 2)]
        mm_base = [sum(phases[:n]) for n in range(K + 2)]
        unit_base = [sum(units[:n]) for n in range(K + 1)]
        subs = [c // SC for c in CHUNKS]
        sub_base = [sum(subs[:n]) for n in range(K + 1)]

        block = ctx.enter_context(nc.Block())

        def loop(eng, count, body, start=0):
            if count > start:
                with eng.Fori(start, count) as i:
                    body(i)

        def merged(eng, k, apply_turn, perm_turn):
            a = CAPS[k] // ROUND
            p = CHUNKS[k + 1] // PTURN if k + 1 < K else 0
            both = min(a, p)

            def two(i):
                for h in range(RING):
                    apply_turn(k, i, h)
                    perm_turn(k + 1, i, h)
            loop(eng, both, two)
            loop(eng, a, lambda i: [apply_turn(k, i, h) for h in range(RING)], both)
            loop(eng, p, lambda i: [perm_turn(k + 1, i, h) for h in range(RING)], both)

        @block.sync
        def _(sp):
            sp.dma_start(rows[0:EP, :], x["row"].rearrange("(p j) -> p j", p=EP)).then_inc(s_rows, 16)
            sp.dma_start(cols[0:EP, :], x["col"].rearrange("(p j) -> p j", p=EP)).then_inc(s_cols, 16)
            sp.dma_start(vals[0:EP, :], x["val"].rearrange("(p j) -> p j", p=EP)).then_inc(s_vals, 16)
            for t, src in ((w1a, x["w1"][0:P, :]), (w1b, x["w1"][P:2 * P, :]), (g1, x["g1"]), (g2, x["g2"]),
                           (pos, x["emb"][0:L, :]), (w2, x["w2"])):
                sp.dma_start(t[:], src).then_inc(s_w, 16)
            sp.dma_start(gb[:], x["gb"].rearrange("(p a) -> p a", a=1)).then_inc(s_w, 16)

            def load_table(dst, src, s):
                v = dst.rearrange("p (b d) -> p b d", d=D)
                sp.dma_start(v[:, 0:FULL, :], src[0:FULL * P, :].rearrange("(b p) d -> p b d", p=P)).then_inc(s, 16)
                sp.dma_start(v[0:LAST, FULL, :], src[FULL * P:N, :]).then_inc(s, 16)

            sp.wait_ge(s_sorted, 1)
            load_table(total, x["emb"], s_emb)
            for dst, src in ((items_i, "items"), (alias_i, "alias"), (inputs_i, "inputs")):
                sp.dma_start(dst, x[src].rearrange("(t p) l -> p t l", p=P)).then_inc(s_ids, 16)
            sp.wait_ge(s_h1, 1)
            sp.dma_start(h1.rearrange("(b p) d -> p b d", p=P),
                         acc.rearrange("p (b d) -> p b d", d=D)).then_inc(s_h1w, 16)
            sp.wait_ge(s_h1w, 16)
            sp.wait_ge(s_total, 1)
            load_table(acc, x["feat"], s_feat)
            comb_v = comb.rearrange("(b p) d -> p b d", p=P)
            for q in range(PIECES):
                w = NBLK // PIECES
                sp.wait_ge(s_comb, q + 1)
                sp.dma_start(comb_v[:, q * w:q * w + w, :],
                             acc[:, q * w * D:(q + 1) * w * D].rearrange("p (b d) -> p b d", d=D)).then_inc(s_combw, 16)

            sp.sem_inc(s_free, 2)

            def store_scores(c):
                i, par = c
                for q in range(OB // OG):
                    m = OG * par + q
                    j = q * OG + OG - 1
                    n = OB * par + j
                    sp.wait_ge(s_scev[0], OB * i + n // 2 + 1)
                    sp.sem_inc(s_staged, 1)
                    sp.wait_ge(s_scev[1], OB * i + (n + 1) // 2)
                    sp.sem_inc(s_staged, 1)
                    w = min(OG * OBW, N - q * OG * OBW)
                    sp.dma_start(out[bass.ds((2 * i + par) * P, P), q * OG * OBW:q * OG * OBW + w],
                                 stage[:, m % 2, 0:w]).then_inc(s_out[m % 2], 16)
                    sp.wait_ge(s_out[m % 2], 16 * (OG * i + m // 2 + 1))
                    sp.sem_inc(s_free, 1)
            with sp.Fori(0, ST // 2) as i:
                store_scores((i, 0))
                store_scores((i, 1))

        @block.gpsimd
        def _(pool):
            kw = dict(allow_small_or_imprecise_dtypes=True)
            pool.iota(iota_bin[:], [[1, NB]], base=0, channel_multiplier=0, **kw).then_inc(s_const, 1)
            pool.iota(iota_q[:], [[1, P]], base=0, channel_multiplier=0, **kw).then_inc(s_const, 1)
            pool.iota(iota_t[:], [[1, CAPMAX]], base=-MID, channel_multiplier=0, **kw).then_inc(s_const, 1)
            pool.iota(iota_r[:], [[1, R]], base=0, channel_multiplier=0, **kw).then_inc(s_const, 1)
            pool.iota(iota_tq[:], [[P, QT]], base=0, channel_multiplier=1, **kw).then_inc(s_const, 1)
            pool.memset(ones_b[:], 1.0).then_inc(s_cz, 1)
            pool.memset(ones_f[:], 1.0).then_inc(s_cz, 1)
            pool.memset(zero_b[:], 0.0).then_inc(s_cz, 1)
            pool.memset(ident[:], 0.0).then_inc(s_cz, 1)
            pool.wait_ge(s_cz, 4)
            pool.affine_select(out=ident[:], in_=ident[:], compare_op=ALU.not_equal, fill=1.0,
                               base=0, pattern=[[-1, P]], channel_multiplier=1).then_inc(s_const, 1)
            pool.affine_select(out=below[:], in_=ones_b[:], compare_op=ALU.is_ge, fill=0.0,
                               base=-1, pattern=[[1, P]], channel_multiplier=-1).then_inc(s_const, 1)
            for k in range(K + 1):
                table = x["emb"] if k < K else h1
                if k == K:
                    pool.wait_ge(s_h1w, 16)

                def turn(i):
                    for h in range(RING):
                        pool.wait_ge(s_idx, idx_base[k] + i * RING + h + 1)
                        pool.sem_inc(s_cz, 1)
                        for u in range(W):
                            n = h * W + u
                            pool.indirect_dma_start(
                                out=gath[:, h, u, :], out_offset=None, in_=table[:, :],
                                in_offset=bass.IndirectOffsetOnAxis(ap=iring[:, n:n + 1], axis=0),
                            ).then_inc(s_g[h], 16)
                loop(pool, phases[k] // RING, turn)
            pool.wait_ge(s_combw, 16 * PIECES)
            with pool.Fori(0, ST // 2) as i:
                for par in range(2):
                    pool.wait_ge(s_sidx, 2 * i + par + 1)
                    pool.sem_inc(s_cz, 1)
                    for l in range(L):
                        pool.indirect_dma_start(
                            out=seq[par][:, l, :], out_offset=None, in_=comb[:, :],
                            in_offset=bass.IndirectOffsetOnAxis(ap=idx50[:, par, l:l + 1], axis=0),
                        ).then_inc(s_seq[par][l // GL], 16)

        CONSTS = 7

        @block.vector
        def _(dve):
            steps = [0]

            def link(ins):
                steps[0] = steps[0] + 1
                ins.then_inc(s_dve, 1)
                dve.wait_ge(s_dve, steps[0])

            def counted_loop(count, per, body):
                start = steps[0]
                with dve.Fori(0, count) as i:
                    steps[0] = start + i * per
                    body(i)
                steps[0] = start + count * per

            def prep(k):
                c, at = CHUNKS[k], slice(COL0[k], COL0[k + 1])
                e = slice(0, EP)
                if k == 0:
                    dve.wait_ge(s_rows, 16)
                link(dve.tensor_scalar(t0[e, 0:c], rows[e, at], 8, None, ALU.arith_shift_right))
                dve.tensor_copy(binb[e, 0:c], t0[e, 0:c])
                link(dve.tensor_scalar(t1[e, 0:c], rows[e, at], R - 1, None, ALU.bitwise_and))
                if k == 0:
                    dve.wait_ge(s_cols, 16)
                link(dve.scalar_tensor_tensor(out=pk[e, 0:c], in0=t1[e, 0:c], scalar=float(1 << COLBITS),
                                              in1=cols[e, at], op0=ALU.mult, op1=ALU.add))
                link(dve.tensor_scalar(t0[e, 0:c], pk[e, 0:c], (1 << LO) - 1, None, ALU.bitwise_and))
                link(dve.tensor_scalar(t1[e, 0:c], pk[e, 0:c], LO, None, ALU.arith_shift_right))
                dve.tensor_scalar(lo[e, 0:c], t0[e, 0:c], 1.0 / 64, None, ALU.mult)
                dve.tensor_scalar(hi[e, 0:c], t1[e, 0:c], float(1 << LO) / 64, None, ALU.mult)
                if k == 0:
                    dve.wait_ge(s_vals, 16)
                link(dve.tensor_copy(vb[e, 0:c], vals[e, at]))
                dve.tensor_copy(v1[e, 0:c], vb[e, 0:c])
                link(dve.tensor_tensor(r1[e, 0:c], vals[e, at], vb[e, 0:c], ALU.subtract))
                link(dve.tensor_copy(vb[e, 0:c], r1[e, 0:c]))
                dve.tensor_copy(v2[e, 0:c], vb[e, 0:c])
                link(dve.tensor_tensor(v3[e, 0:c], r1[e, 0:c], vb[e, 0:c], ALU.subtract))

            def rank(k):
                c, e = CHUNKS[k], slice(0, EP)
                G = c // GS
                cnt = view(cnt_w, [cnt_w], F32, at=cnt_at)[:, 0:NB * G]
                inc = view(cnt_w, [cnt_w], F32, at=inc_at)[:, 0:NB * G]
                rst = view(cnt_w, [cnt_w], F32, at=rst_at)[:, 0:NB * G]
                cnt3, inc3, rst3 = (v.rearrange("p (b g) -> p b g", g=G) for v in (cnt, inc, rst))

                def onehot(i):
                    at = bass.ds(i * SC, SC)
                    dve.tensor_tensor(oh[e, at, :], binb[e, at].unsqueeze(2).to_broadcast([EP, SC, NB]),
                                      iota_bin[e, :].unsqueeze(1).to_broadcast([EP, SC, NB]),
                                      ALU.is_equal).then_inc(s_oh, 1)
                loop(dve, subs[k], onehot)
                link(dve.memset(rst, 1.0))
                link(dve.memset(rst3[:, :, 0:1], 0.0))
                dve.wait_ge(s_ctc, 1 + sub_base[k + 1])
                link(dve.tensor_tensor_scan(inc, rst, cnt, 0.0, ALU.mult, ALU.add))
                link(dve.tensor_scalar(tiles_i[:].unsqueeze(2), inc3[:, :, G - 1:G], float(P - 1), None, ALU.add))
                link(dve.tensor_scalar(tiles_i[:], tiles_i[:], 7, None, ALU.arith_shift_right))
                link(dve.tensor_copy(tiles_f[:], tiles_i[:]))
                link(dve.tensor_tensor_scan(tiles_inc[:], ones_f[:, 0:NB], tiles_f[:], 0.0, ALU.mult, ALU.add))
                link(dve.tensor_tensor(base[:], tiles_inc[:], tiles_f[:], ALU.subtract))
                link(dve.tensor_scalar(base[:], base[:], float(P), None, ALU.mult))
                link(dve.tensor_tensor(inc, inc, cnt, ALU.subtract))
                dve.tensor_tensor(cnt3, inc3, base[:].unsqueeze(2).to_broadcast([P, NB, G]),
                                  ALU.add).then_inc(s_cum, 1)
                link(dve.tensor_tensor(past[:], iota_tq[:].unsqueeze(2).to_broadcast([P, QT, NB - 1]),
                                       tiles_inc[:, 0:NB - 1].unsqueeze(1).to_broadcast([P, QT, NB - 1]),
                                       ALU.is_ge))
                link(dve.tensor_reduce(bin_of[:], past[:], AX.X, ALU.add))
                dve.tensor_scalar(bin_of[:], bin_of[:], float(R), None, ALU.mult).then_inc(s_binof, 1)
                dve.wait_ge(s_row1, k + 1)
                dve.tensor_copy(tab[0:1, TILE0[k]:TILE0[k + 1]], ps_rank[1][0:1, 0:CAPS[k]]).then_inc(s_tab, 1)
                link(dve.memset(before[e, :, 0, :], 0.0))

                def sub_batch(i):
                    for s in range(1, GS):
                        ins = dve.tensor_tensor(before[e, :, s, :], before[e, :, s - 1, :],
                                                oh[e, bass.ds(i * SC, SC), :].rearrange(
                                                    "p (g s) b -> p g s b", s=GS)[:, :, s - 1, :], ALU.add)
                        if s < GS - 1:
                            link(ins)
                    ins.then_inc(s_before, 1)
                    for g in range(SUB):
                        n = g % 2
                        dve.wait_ge(s_rank, sub_base[k] * SUB + i * SUB + g + 1)
                        ins = dve.tensor_tensor(
                            picked[e, n], ps_rank[n][e, 0:GS * NB].rearrange("p (s b) -> p s b", b=NB),
                            oh[e, bass.ds(i * SC + g * GS, GS), :], ALU.mult)
                        ins.then_inc(s_pick, 1)
                        dve.wait_ge(s_pick, 2 + sub_base[k] * SUB + i * SUB + g + 1)
                        dve.tensor_reduce(r1[e, bass.ds(i * SC + g * GS, GS)], picked[e, n], AX.X, ALU.add)
                counted_loop(subs[k], GS - 2, sub_batch)
                link(dve.memset(picked[0:1, 0, 0, 0:1], 0.0))
                link(dve.tensor_copy(pk[e, 0:c], r1[e, 0:c]))
                link(dve.tensor_scalar(t0[e, 0:c], pk[e, 0:c], 7, None, ALU.arith_shift_right))
                link(dve.tensor_scalar(t1[e, 0:c], pk[e, 0:c], P - 1, None, ALU.bitwise_and))
                dve.tensor_scalar(tf[e, 0:c], t0[e, 0:c], float(-MID), None, ALU.add)
                link(dve.tensor_copy(qf[e, 0:c], t1[e, 0:c]))

            def perm_turn(k, i, h):
                e, n, cap = slice(0, EP), h % 2, CAPS[k]
                dve.wait_ge(s_pm, unit_base[k] + i * RING + h + 1)
                for u in range(PW):
                    at = bass.ds(i * PTURN + h * PW + u, 1)
                    dve.tensor_scalar(ohq[e, n, u, :], iota_q[e, :], qf[e, at], None, ALU.is_equal)
                    dve.tensor_scalar(ohi[e, n, u, 0:P], iota_q[e, :], qf[e, at], lo[e, at],
                                      ALU.is_equal, ALU.mult)
                    dve.tensor_scalar(ohi[e, n, u, P:2 * P], iota_q[e, :], qf[e, at], hi[e, at],
                                      ALU.is_equal, ALU.mult)
                    ins = dve.tensor_scalar(oht[e, n, u, 0:cap], iota_t[e, 0:cap], tf[e, at], None,
                                            ALU.is_equal)
                ins.then_inc(s_pd, 1)

            def evacuate(k):
                cap, at = CAPS[k], slice(TILE0[k], TILE0[k + 1])
                dve.wait_ge(s_pz, k + 1)
                word = arena[:, cnt_at:cnt_at + cap].bitcast(I32)
                part = arena[:, inc_at:inc_at + cap].bitcast(I32)
                link(dve.tensor_scalar(word, ps_idx[:, 0:cap], 64.0, None, ALU.mult))
                link(dve.tensor_scalar(idx_s[:, at], word, (1 << COLBITS) - 1, None, ALU.bitwise_and))
                link(dve.tensor_scalar(part, word, COLBITS, None, ALU.arith_shift_right))
                link(dve.tensor_copy(row_s[:, at], part))
                link(dve.tensor_copy(val_s[:, at], ps_val[:, 0:cap]))
                link(dve.memset(picked[0:1, 0, 0, 0:1], 0.0))
                dve.sem_inc(s_ev, 1)

            def fill(t, h):
                dve.tensor_copy(iring[:, h * W:h * W + W], idx_s[:, bass.ds(t, W)]).then_inc(s_idx, 1)

            def make_hot(t, n, u):
                at = bass.ds(t, 1)
                return dve.tensor_scalar(hot[:, n, u, :], iota_r[:], row_s[:, at], val_s[:, at],
                                         ALU.is_equal, ALU.mult)

            def start_apply(k):
                first = TILE0[k] if k < K else 0
                if k:
                    dve.wait_ge(s_idx, idx_base[k])
                    dve.wait_ge(s_hot, hot_base[k])
                for h in range(RING):
                    fill(first + h * W, h)
                for n in range(2):
                    for u in range(W):
                        ins = make_hot(first + n * W + u, n, u)
                    ins.then_inc(s_hot, 1)

            def apply_turn(k, i, h):
                n = h % 2
                first = TILE0[k] if k < K else 0
                t = i * ROUND + (first + h * W)
                done = mm_base[k] * W
                offs = [dve.value_load(tab[0:1, bass.ds(t + u, 1)], min_val=0, max_val=(NB - 1) * R)
                        for u in range(W)]
                dve.wait_ge(s_mm, mm_base[k] + i * RING + h + 1)
                fill(t + ROUND, h)
                for u in range(W):
                    part = target(k)[:, bass.ds(offs[u], R)]
                    dve.wait_ge(s_acc, 1 + done + i * ROUND + h * W + u)
                    ins = dve.tensor_tensor(part, part, ps_app[n][:, u, :], ALU.add)
                    ins.then_inc(s_acc, 1)
                    last = make_hot(t + 2 * W + u, n, u)
                last.then_inc(s_hot, 1)
                dve.wait_ge(s_acc, 1 + done + i * ROUND + h * W + W)
                dve.sem_inc(s_add, 1)

            def target(k):
                return acc if k < K else total

            link(dve.memset(acc, 0.0))
            link(dve.memset(idx_s, 0))
            link(dve.memset(row_s, 0.0))
            link(dve.memset(val_s, 0.0))
            link(dve.memset(tab[:], 0))
            dve.sem_inc(s_acc, 1)
            dve.sem_inc(s_add, 2)
            dve.sem_inc(s_pick, 2)
            dve.wait_ge(s_const, CONSTS)
            prep(0)
            rank(0)
            loop(dve, CHUNKS[0] // PTURN, lambda i: [perm_turn(0, i, h) for h in range(RING)])
            evacuate(0)
            for k in range(K):
                start_apply(k)
                if k + 1 < K:
                    prep(k + 1)
                    rank(k + 1)
                else:
                    link(dve.memset(total[:, FULL * D:NBLK * D], 0.0))
                    dve.sem_inc(s_sorted, 1)
                merged(dve, k, apply_turn, perm_turn)
                if k + 1 < K:
                    evacuate(k + 1)
            dve.sem_inc(s_h1, 1)
            dve.wait_ge(s_emb, 32)
            dve.tensor_tensor(total, total, acc, ALU.add).then_inc(s_total, 1)
            dve.wait_ge(s_ids, 48)
            link(dve.tensor_copy(items_f, items_i))
            link(dve.tensor_scalar(wrap, items_f, 0.0, float(N), ALU.is_lt, ALU.mult))
            link(dve.tensor_tensor(items_f, items_f, wrap, ALU.add))
            link(dve.tensor_scalar(items_f, items_f, 0.0, float(N - 1), ALU.max, ALU.min))
            link(dve.tensor_copy(alias_f, alias_i))
            link(dve.tensor_scalar(mask, inputs_i, 0.0, None, ALU.not_equal))
            link(dve.tensor_reduce(n_in[:], mask, AX.X, ALU.add))
            link(dve.reciprocal(cinv[:], n_in[:]))
            link(dve.memset(idx_f, 0.0))
            dve.wait_ge(s_total, 1)
            dve.sem_inc(s_sel, 1)
            start_apply(K)

            def select(i):
                dve.wait_ge(s_sel, ST * i + 1)
                for t in range(ST):
                    dve.scalar_tensor_tensor(out=scrap[:, t, :], in0=iota_r[:, 0:L], scalar=alias_f[:, t, bass.ds(i, 1)],
                                             in1=items_f[:, t, :], op0=ALU.is_equal, op1=ALU.mult,
                                             accum_out=idx_f[:, t, bass.ds(i, 1)]).then_inc(s_sel, 1)
            loop(dve, L, lambda i: [select(i), [apply_turn(K, i, h) for h in range(RING)]])
            loop(dve, phases[K] // RING, lambda i: [apply_turn(K, i, h) for h in range(RING)], L)

            dve.wait_ge(s_sel, 1 + ST * L)
            dve.wait_ge(s_feat, 32)
            w = NBLK // PIECES * D
            for q in range(PIECES):
                at = slice(q * w, q * w + w)
                dve.scalar_tensor_tensor(out=acc[:, at], in0=total[:, at], scalar=1.0 / 3, in1=acc[:, at],
                                         op0=ALU.mult, op1=ALU.add).then_inc(s_comb, 1)

            def fill_session(t, par):
                dve.tensor_copy(idx50[:, par, :], idx_f[:, t, :] if isinstance(t, int) else
                                idx_f[:, bass.ds(t, 1), :].rearrange("p a l -> p (a l)")).then_inc(s_sidx, 1)
            fill_session(0, 0)
            dve.wait_ge(s_combw, 16 * PIECES)
            fill_session(1, 1)
            dve.wait_ge(s_rroot, 1)
            link(dve.tensor_scalar(row_n[:], row_n[:], 1.0 / 3, EPS, ALU.mult, ALU.max))
            link(dve.reciprocal(row_n[:], row_n[:]))
            link(dve.tensor_scalar(row_n[:], row_n[:], 1.0 / 3, None, ALU.mult))
            total3 = total.rearrange("p (b d) -> p b d", d=D)

            def scale_rows(first, count, n, r):
                wait(dve, s_turned, r - 1)
                dve.tensor_tensor(turn_in[:, n, 0:count, :], total3[:, bass.ds(first, count), :],
                                  row_n[:, bass.ds(first, count)].unsqueeze(2).to_broadcast([P, count, D]),
                                  ALU.mult).then_inc(s_scaled, 1)
            scale_rows(0, SG, 0, 0)
            scale_rows(SG, SG, 1, 1)

            def scale_two(i):
                for n in range(2):
                    scale_rows(i * 2 * SG + n * SG, SG, n, 2 * i + n)
            loop(dve, TR // 2, scale_two, 1)
            scale_rows(TR * SG, NBLK - TR * SG, 0, TR)

            def session(t, par, c):
                for g, (l0, wl) in enumerate(SGS):
                    n = (par * NG + g) % 2
                    dve.wait_ge(s_tr, t * NG + g + 1)
                    wait(dve, s_m1, t * NG + g - 1)
                    dve.tensor_copy(seq_t[:, n, 0:wl * P], ps_turn[n][:, 0:wl * P]).then_inc(s_seqt, 1)
                    for l in range(l0, l0 + wl):
                        m = mask[:, bass.ds(t, 1), l]
                        if l == 0:
                            ins = dve.tensor_scalar(hs, seq[par][:, l, :], m, None, ALU.mult)
                        else:
                            ins = dve.scalar_tensor_tensor(out=hs, in0=seq[par][:, l, :], scalar=m, in1=hs,
                                                           op0=ALU.mult, op1=ALU.add)
                        link(ins)
                    if c:
                        for j in (2 * g, 2 * g + 1):
                            if j < OB:
                                evacuate_scores(dve, 0, c, j)
                wait(dve, s_ht, t)
                dve.tensor_scalar(hs_n, hs, cinv[:, bass.ds(t, 1)], None, ALU.mult).then_inc(s_hsn, 1)
                dve.wait_ge(s_bt, t * NG + NG)
                link(dve.tensor_tensor(beta, ps_beta, mask[:, bass.ds(t, 1), :].rearrange("p a l -> p (a l)"), ALU.mult))
                for l in range(L):
                    b = beta[:, l:l + 1]
                    if l == 0:
                        ins = dve.tensor_scalar(sess, seq[par][:, l, :], b, None, ALU.mult)
                    else:
                        ins = dve.scalar_tensor_tensor(out=sess, in0=seq[par][:, l, :], scalar=b, in1=sess,
                                                       op0=ALU.mult, op1=ALU.add)
                    link(ins)
                dve.sem_inc(s_sess, 1)
                fill_session(t + 2, par) if not (isinstance(t, int) and t + 2 > ST) else None
                dve.scalar_tensor_tensor(out=sess_sq, in0=sess, scalar=1.0, in1=sess, op0=ALU.mult, op1=ALU.mult,
                                         accum_out=ss[:, par:par + 1]).then_inc(s_ss, 1)
                dve.wait_ge(s_root, t + 1)
                link(dve.tensor_scalar(rsc[:, par:par + 1], root[:, par:par + 1], EPS, None, ALU.max))
                link(dve.reciprocal(rsc[:, par:par + 1], rsc[:, par:par + 1]))
                link(dve.tensor_scalar(rsc[:, par:par + 1], rsc[:, par:par + 1], W_K, None, ALU.mult))
                dve.sem_inc(s_rsc, 1)
            per = 2 * L + 1 + 3
            first = steps[0]

            def step(t, par, c):
                steps[0] = first + t * per
                session(t, par, c)
            session_steps(dve, step)
            steps[0] = first + ST * per
            for j in range(OB):
                evacuate_scores(dve, 0, LASTC, j)

        @block.tensor
        def _(pe):
            pe.wait_ge(s_const, CONSTS)
            pe.sem_inc(s_pm, 2)
            pe.wait_ge(s_w, 16 * 7)
            pe.transpose(ps_app[0][:, 0, 0:P], g1[:], ident[:])
            pe.transpose(ps_app[0][:, 0, P:2 * P], g2[:], ident[:])
            pe.transpose(ps_app[0][:, 1, 0:L], pos[:], ident[0:L, 0:L]).then_inc(s_wt, 1)
            pe.wait_ge(s_wtc, 3)
            pe.matmul(ps_app[0][:, 1, L:2 * L], w1a[:], pos_t[:], start=True, stop=True).then_inc(s_wt, 1)
            pe.wait_ge(s_wtc, 4)
            def rank(k):
                c = CHUNKS[k]
                G = c // GS
                cnt3 = view(cnt_w, [cnt_w], F32, at=cnt_at)[:, 0:NB * G].rearrange("p (b g) -> p b g", g=G)
                pe.wait_ge(s_pick, 2 + sub_base[k] * SUB)

                def counts(i):
                    pe.wait_ge(s_oh, sub_base[k] + i + 1)
                    pe.wait_ge(s_ctc, 1 + sub_base[k] + i)
                    o = oh[0:EP, bass.ds(i * SC, SC), :].rearrange("p (g s) b -> p g s b", s=GS)
                    for s in range(GS):
                        ins = pe.matmul(ps_rank[0][:, 0:SUB * NB], ones_b[0:EP, :], o[:, :, s, :],
                                        start=(s == 0), stop=(s == GS - 1))
                    ins.then_inc(s_ct, 1)
                loop(pe, subs[k], counts)
                pe.wait_ge(s_binof, k + 1)
                for q in range(-(-CAPS[k] // P)):
                    w = min(P, CAPS[k] - q * P)
                    ins = pe.matmul(ps_rank[1][0:1, q * P:q * P + w], bin_of[:, q:q + 1], ident[:, 0:w],
                                    start=True, stop=True)
                ins.then_inc(s_row1, 1)
                pe.wait_ge(s_cum, k + 1)
                pe.wait_ge(s_tab, k + 1)

                def sub_batch(i):
                    pe.wait_ge(s_before, sub_base[k] + i + 1)
                    for g in range(SUB):
                        n = g % 2
                        pe.wait_ge(s_pick, sub_base[k] * SUB + i * SUB + g + 1)
                        dst = ps_rank[n][0:EP, 0:GS * NB]
                        pe.matmul(dst, below[0:EP, 0:EP], oh[0:EP, bass.ds(i * SC + g * GS, GS), :],
                                  start=True, stop=False)
                        pe.matmul(dst, ones_b[0:EP, 0:EP], before[0:EP, g, :, :], start=False, stop=False)
                        cum = cnt3[0:1, :, bass.ds(i * SUB + g, 1)].rearrange("p b g -> p g b")
                        pe.matmul(dst, ones_f[0:1, 0:EP], cum.to_broadcast([1, GS, NB]),
                                  start=False, stop=True).then_inc(s_rank, 1)
                loop(pe, subs[k], sub_batch)

            def open_banks(k):
                if k:
                    pe.wait_ge(s_ev, k)
                for b in (ps_idx, ps_val):
                    pe.matmul(b[:, 0:CAPS[k]], zero_b[:, :], iota_t[:, 0:CAPS[k]], start=True, stop=False,
                              skip_group_check=True)

            def perm_turn(k, i, h):
                n, cap = h % 2, CAPS[k]
                pe.wait_ge(s_pa, unit_base[k] + i * RING + h + 1)
                for u in range(PW):
                    o = oht[0:EP, n, u, 0:cap]
                    for m in range(2):
                        pe.matmul(ps_idx[:, 0:cap], ohi[0:EP, n, u, m * P:m * P + P], o,
                                  start=False, stop=False, skip_group_check=True)
                    for m in range(3):
                        ins = pe.matmul(ps_val[:, 0:cap], ohv[0:EP, n, u, m * P:m * P + P], o,
                                        start=False, stop=False, skip_group_check=True)
                ins.then_inc(s_pm, 1)

            def close_banks(k):
                for b in (ps_idx, ps_val):
                    ins = pe.matmul(b[:, 0:CAPS[k]], zero_b[:, :], iota_t[:, 0:CAPS[k]], start=False, stop=True,
                                    skip_group_check=True)
                ins.then_inc(s_pz, 1)

            def apply_turn(k, i, h):
                n = h % 2
                used = mm_base[k] // RING * 64
                pe.wait_ge(s_hot, hot_base[k] + i * RING + h + 1)
                pe.wait_ge(s_g[h], used + i * 64 + 64)
                pe.wait_ge(s_add, mm_base[k] + i * RING + h + 1)
                for u in range(W):
                    for r in range(R // P):
                        ins = pe.matmul(ps_app[n][:, u, r * P:r * P + P], hot[:, n, u, r * P:r * P + P],
                                        gath[:, h, u, :], start=True, stop=True)
                ins.then_inc(s_mm, 1)

            rank(0)
            open_banks(0)
            loop(pe, CHUNKS[0] // PTURN, lambda i: [perm_turn(0, i, h) for h in range(RING)])
            close_banks(0)
            for k in range(K):
                if k + 1 < K:
                    rank(k + 1)
                    open_banks(k + 1)
                merged(pe, k, apply_turn, perm_turn)
                if k + 1 < K:
                    close_banks(k + 1)
            loop(pe, phases[K] // RING, lambda i: [apply_turn(K, i, h) for h in range(RING)])

            def turn_rows(count, n, r):
                pe.wait_ge(s_scaled, r + 1)
                wait(pe, s_norm, r - 1)
                for b in range(count):
                    ins = pe.transpose(ps_turn[n][:, b * P:b * P + P], turn_in[:, n, b, :], ident[:])
                ins.then_inc(s_turned, 1)
            turn_rows(SG, 0, 0)
            turn_rows(SG, 1, 1)
            loop(pe, TR // 2, lambda i: [turn_rows(SG, n, 2 * i + n) for n in range(2)], 1)
            turn_rows(NBLK - TR * SG, 0, TR)
            pe.wait_ge(s_norm, TR + 1)

            def scores(c, j):
                i, par = c
                b, n, at, w = score_block(c, j)
                if j == 0:
                    pe.wait_ge(s_sstc, 2 * i + par + 1)
                wait(pe, s_scev[b], n - 1)
                pe.matmul(ps_score[b][:, 0:w], sess_t[:, par, :], total[:, at:at + w],
                          start=True, stop=True).then_inc(s_sc[b], 1)

            def session(t, par, c):
                half = t // 2 if isinstance(t, int) else c[0] + (1 - par)

                def hidden(g):
                    l0, wl = SGS[g]
                    pe.wait_ge(s_seqt, t * NG + g + 1)
                    wait(pe, s_psm, t * 2 * NG + g - 1)
                    pe.matmul(ps_hid[g % 2][:, 0:wl * P], w1b[:], seq_t[:, (par * NG + g) % 2, 0:wl * P],
                              start=True, stop=True).then_inc(s_m1, 1)
                for g, (l0, wl) in enumerate(SGS):
                    n = (par * NG + g) % 2
                    wait(pe, s_seqt, t * NG + g - 1)
                    for l in range(l0, l0 + wl):
                        if l % GL == 0:
                            pe.wait_ge(s_seq[par][l // GL], 16 * GL * (half + 1))
                        ins = pe.transpose(ps_turn[n][:, (l - l0) * P:(l - l0 + 1) * P], seq[par][:, l, :], ident[:])
                    ins.then_inc(s_tr, 1)
                    if g:
                        hidden(g - 1)
                    if c:
                        for j in (2 * g, 2 * g + 1):
                            if j < OB:
                                scores(c, j)
                hidden(NG - 1)
                pe.wait_ge(s_hsn, t + 1)
                pe.transpose(ps_mean, hs_n, ident[:]).then_inc(s_ht, 1)
                pe.wait_ge(s_htc, t + 1)

                def gates(g):
                    l0, wl = SGS[g]
                    pe.wait_ge(s_psm, t * 2 * NG + NG + g + 1)
                    n = (par * NG + g) % 2
                    for l in range(l0, l0 + wl):
                        ins = pe.matmul(ps_beta[:, l:l + 1], gate[:, n, (l - l0) * P:(l - l0 + 1) * P], w2[:],
                                        start=True, stop=True)
                    ins.then_inc(s_bt, 1)
                for g, (l0, wl) in enumerate(SGS):
                    use = NG + g
                    pe.wait_ge(s_psm, t * 2 * NG + max(g + 1, use - 1))
                    dst = ps_hid[use % 2][:, 0:wl * P]
                    pe.matmul(dst, g1_t[:], nh[:, l0 * P:(l0 + wl) * P], start=True, stop=False)
                    pe.matmul(dst, g2_t[:], hs_t.unsqueeze(1).to_broadcast([P, wl, P]), start=False,
                              stop=True).then_inc(s_z, 1)
                    if g:
                        gates(g - 1)
                gates(NG - 1)
                pe.wait_ge(s_sess, t + 1)
                pe.transpose(ps_sess, sess, ident[:]).then_inc(s_sst, 1)
            session_steps(pe, session)
            for j in range(OB):
                scores(LASTC, j)

        @block.scalar
        def _(act):
            act.sem_inc(s_ctc, 1)

            def counts(k):
                G = CHUNKS[k] // GS
                cnt3 = view(cnt_w, [cnt_w], F32, at=cnt_at)[:, 0:NB * G].rearrange("p (b g) -> p b g", g=G)

                def copy(i):
                    act.wait_ge(s_ct, sub_base[k] + i + 1)
                    act.activation(cnt3[:, :, bass.ds(i * SUB, SUB)],
                                   ps_rank[0][:, 0:SUB * NB].rearrange("p (g b) -> p b g", b=NB),
                                   ACT.Copy).then_inc(s_ctc, 1)
                loop(act, subs[k], copy)

            def perm_turn(k, i, h):
                n, e = h % 2, slice(0, EP)
                act.wait_ge(s_pd, unit_base[k] + i * RING + h + 1)
                for u in range(PW):
                    at = bass.ds(i * PTURN + h * PW + u, 1)
                    for m, v in enumerate((v1, v2, v3)):
                        ins = act.activation(ohv[e, n, u, m * P:m * P + P], ohq[e, n, u, :], ACT.Copy,
                                             scale=v[e, at])
                ins.then_inc(s_pa, 1)

            act.wait_ge(s_wt, 1)
            act.activation(g1_t[:], ps_app[0][:, 0, 0:P], ACT.Copy).then_inc(s_wtc, 1)
            act.activation(g2_t[:], ps_app[0][:, 0, P:2 * P], ACT.Copy).then_inc(s_wtc, 1)
            act.activation(pos_t[:], ps_app[0][:, 1, 0:L], ACT.Copy).then_inc(s_wtc, 1)
            act.wait_ge(s_wt, 2)
            act.activation(pos_w[:], ps_app[0][:, 1, L:2 * L], ACT.Copy).then_inc(s_wtc, 1)
            for k in range(K):
                counts(k)
                loop(act, CHUNKS[k] // PTURN, lambda i: [perm_turn(k, i, h) for h in range(RING)])

            act.wait_ge(s_comb, PIECES)
            total3 = total.rearrange("p (b d) -> p b d", d=D)
            act.sem_inc(s_rss, 1)

            def squares(i):
                act.wait_ge(s_rss, i + 1)
                act.activation(square, total3[:, bass.ds(i, 1), :].rearrange("p a d -> p (a d)"), ACT.Square,
                               accum_out=row_ss[:, bass.ds(i, 1)]).then_inc(s_rss, 1)
            loop(act, NBLK, squares)
            act.wait_ge(s_rss, NBLK + 1)
            act.activation(row_n[:], row_ss[:], ACT.Sqrt).then_inc(s_rroot, 1)

            def place(first, count, n, r):
                act.wait_ge(s_turned, r + 1)
                act.activation(total[:, bass.ds(first * P, count * P)], ps_turn[n][:, 0:count * P],
                               ACT.Copy).then_inc(s_norm, 1)
            loop(act, TR // 2, lambda i: [place(i * 2 * SG + n * SG, SG, n, 2 * i + n) for n in range(2)])
            place(TR * SG, NBLK - TR * SG, 0, TR)

            def session(t, par, c):
                for g, (l0, wl) in enumerate(SGS):
                    act.wait_ge(s_m1, t * NG + g + 1)
                    for l in range(l0, l0 + wl):
                        ins = act.activation(nh[:, l * P:l * P + P], ps_hid[g % 2][:, (l - l0) * P:(l - l0 + 1) * P],
                                             ACT.Tanh, bias=pos_w[:, L - 1 - l:L - l])
                    ins.then_inc(s_psm, 1)
                    if c:
                        for j in (2 * g, 2 * g + 1):
                            if j < OB:
                                evacuate_scores(act, 1, c, j)
                act.wait_ge(s_ht, t + 1)
                act.activation(hs_t, ps_mean, ACT.Copy).then_inc(s_htc, 1)
                for g, (l0, wl) in enumerate(SGS):
                    act.wait_ge(s_z, t * NG + g + 1)
                    wait(act, s_bt, t * NG + g - 1)
                    act.activation(gate[:, (par * NG + g) % 2, 0:wl * P], ps_hid[(NG + g) % 2][:, 0:wl * P],
                                   ACT.Sigmoid, bias=gb[:]).then_inc(s_psm, 1)
                act.wait_ge(s_sst, t + 1)
                act.activation(sess_t[:, par, :], ps_sess, ACT.Copy).then_inc(s_sstc, 1)
                act.wait_ge(s_ss, t + 1)
                act.activation(root[:, par:par + 1], ss[:, par:par + 1], ACT.Sqrt).then_inc(s_root, 1)
            session_steps(act, session)
            for j in range(OB):
                evacuate_scores(act, 1, LASTC, j)


_INS = {"items": "r_items", "inputs": "r_inputs", "alias": "r_alias_inputs", "feat": "L0_rec_item_features",
        "row": "L0_rec_adj_row", "col": "L0_rec_adj_col", "val": "L0_rec_adj_val", "emb": "L0_rec_emb",
        "w1": "L0_rec_w_1", "w2": "L0_rec_w_2", "g1": "L0_rec_glu1_w", "gb": "L0_rec_glu1_b", "g2": "L0_rec_glu2_w"}


def kernel(**inputs):
    import concourse.bacc as bacc
    from concourse.bass_utils import run_bass_kernel_spmd

    nc = bacc.Bacc("TRN2", target_bir_lowering=False, num_devices=1)
    arrays, x = {}, {}
    for name, full in _INS.items():
        a = np.ascontiguousarray(inputs[full])
        arrays[f"in_{name}"] = a
        x[name] = nc.dram_tensor(f"in_{name}", a.shape, mybir.dt.from_np(a.dtype), kind="ExternalInput").ap()
    out = nc.dram_tensor("scores", (B, N), F32, kind="ExternalOutput").ap()
    build(nc, x, out)
    r = run_bass_kernel_spmd(nc, [arrays], core_ids=[0])
    return r.results[0]["scores"]
```

```python
from contextlib import ExitStack

import numpy as np

import concourse.bass as bass
from concourse import mybir

F32 = mybir.dt.float32
BF16 = mybir.dt.bfloat16
F16 = mybir.dt.float16
I32 = mybir.dt.int32
ALU = mybir.AluOpType
ACT = mybir.ActivationFunctionType
AX = mybir.AxisListType

P = 128
N, D = 12501, 128
E = 150000
EP = 125
EC = E // EP
R = 256
NB = -(-N // R)
NBLK = NB * R // P
FULL, LAST = N // P, N % P
BG = 7
CHUNKS = [112, 176, 256, 320, 336]
assert sum(CHUNKS) == EC and NB % BG == 0
W = 4
RING = 4
PW = 4
AHEAD = 2
ROUND = W * RING
PTURN = PW * RING
CAPS = [-(-((EP * c + NB * (P - 1)) // P) // ROUND) * ROUND for c in CHUNKS]
CMAX, CAPMAX = max(CHUNKS), max(CAPS)
TILES = sum(CAPS)
TPAD = TILES + ROUND
TILE0 = [sum(CAPS[:k]) for k in range(len(CAPS) + 1)]
COL0 = [sum(CHUNKS[:k]) for k in range(len(CHUNKS) + 1)]
K = len(CHUNKS)
MID = CAPMAX // 2
LO = 11
COLBITS = 14
QT = -(-CAPMAX // P)
B, L = 1024, 50
ST = B // P
OBW = 512
OB = -(-N // OBW)
OG = 5
SG = 4
SGS = [(l, min(SG, L - l)) for l in range(0, L, SG)]
NG = len(SGS)
GL = 10
PIECES = 7
TR = NBLK // SG
W_K, EPS = 12.0, 1e-12
assert OB == 5 * OG and NBLK % PIECES == 0 and ST % 2 == 0


def build(nc, x, out):
    ctx = ExitStack()
    with ctx:
        def sb(name, shape, dt):
            return ctx.enter_context(nc.sbuf_tensor(name, shape, dt))

        def sem(name):
            return ctx.enter_context(nc.semaphore(name))

        WORDS = 48640
        arena = sb("arena", [P, WORDS], F32)
        top = [0]

        def view(words, shape, dt, at=None, parts=P):
            start = top[0] if at is None else at
            if at is None:
                top[0] += words
            assert start + words <= WORDS, (start, words)
            v = arena[0:parts, start:start + words]
            if dt is not F32:
                v = v.bitcast(dt)
            names = " ".join("abcd"[:len(shape)])
            sizes = {"abcd"[n]: s for n, s in enumerate(shape)}
            if len(shape) > 1:
                v = v.rearrange(f"p ({names}) -> p {names}", **sizes)
            return v

        ACCW = NBLK * D
        acc = view(ACCW, [ACCW], F32)[:, 0:NBLK * D]
        low = top[0]
        rows = view(EC, [EC], I32)
        cols = view(EC, [EC], I32)
        vals = view(EC, [EC], F32)
        CPAD = CMAX + AHEAD * PW
        lo, hi, v1, v2, v3, qf, tf, t0, t1, pk = (view(CPAD, [CPAD], F32 if n < 7 else I32) for n in range(10))
        r1 = view(CMAX, [CMAX], F32)
        binb = view(CMAX // 2, [CMAX], BF16)
        vb = view(CMAX // 2, [CMAX], BF16)
        oh = view(CMAX * NB // 2, [NB * CMAX], BF16)
        cnt_at = top[0]
        seen = view(CMAX * NB // 2, [NB * CMAX], F16, at=cnt_at)
        picked = view(BG * CMAX, [BG, CMAX], F32, at=cnt_at + CMAX * NB // 2)
        oht = view(RING * PW * CAPMAX // 2, [RING, PW, CAPMAX], BF16)
        ohq = view(RING * PW * P // 2, [RING, PW, P], BF16)
        ohi = view(RING * PW * 2 * P // 2, [RING, PW, 2 * P], F16)
        ohv = view(RING * PW * 3 * P // 2, [RING, PW, 3 * P], BF16)
        word_at, part_at = cnt_at, cnt_at + CAPMAX
        top[0] = max(top[0], cnt_at + CMAX * NB // 2 + BG * CMAX)
        high = top[0] = max(top[0], low + ACCW + 2 * L * P + (5 * ST + 2) * L)
        idx_s = view(TPAD, [TPAD], I32)
        row_s = view(TPAD, [TPAD], F32)
        val_s = view(TPAD, [TPAD], F32)
        gath = view(RING * W * D, [RING, W, D], F32)
        hot = view(2 * W * R, [2, W, R], F32)

        total = view(ACCW, [ACCW], F32, at=low)
        seq = [view(L * D, [L, D], F32, at=a) for a in (0, low + ACCW)]
        stage = view(2 * OG * OBW, [2, OG * OBW], F32, at=L * D)
        nh_at = low + ACCW + L * D
        nh = view(L * P, [L * P], F32, at=nh_at)
        items_i, alias_i, inputs_i = (view(ST * L, [ST, L], I32, at=nh_at + n * ST * L) for n in range(3))
        wrap = view(ST * L, [ST, L], F32, at=nh_at + 3 * ST * L)
        top[0] = nh_at + L * P
        items_f = view(ST * L, [ST, L], F32)
        alias_f = view(ST * L, [ST, L], F32)
        mask = view(ST * L, [ST, L], F32)
        idx_f = view((ST + 2) * L, [ST + 2, L], F32)
        scrap = view(ST * L, [ST, L], F32)
        assert top[0] <= high
        top[0] = high
        seq_t = view(2 * SG * P, [2, SG * P], F32)
        gate = view(2 * SG * P, [2, SG * P], F32)
        turn_in = view(2 * SG * P, [2, SG, P], F32)
        square = view(D, [D], F32)
        hs = view(SG * D, [SG, D], F32)
        hs_n = view(D, [D], F32)
        hs_t = view(P, [P], F32)
        sess = view(SG * D, [SG, D], F32)
        sess_n = view(D, [D], F32)
        sess_t = view(2 * P, [2, P], F32)
        sess_sq = view(D, [D], F32)
        beta = view(L, [L], F32)

        tiles_i = sb("tiles_i", [P, NB], I32)
        tiles_f = sb("tiles_f", [P, NB], F32)
        tiles_inc = sb("tiles_inc", [P, NB], F32)
        base = sb("base", [P, NB], F32)
        upto = sb("upto", [P, NB], F32)
        hist = sb("hist", [P, NB], F32)
        past = sb("past", [P, QT, NB - 1], F32)
        bin_of = sb("bin_of", [P, QT], F32)
        tab = sb("tab", [1, TPAD], I32)
        iring = sb("iring", [P, RING * W], I32)
        idx50 = sb("idx50", [P, 2, L], I32)
        w1a, w1b, g1, g2, g1_t, g2_t = (sb(n, [P, P], F32) for n in ("w1a", "w1b", "g1", "g2", "g1_t", "g2_t"))
        w2, gb = sb("w2", [P, 1], F32), sb("gb", [P, 1], F32)
        pos = sb("pos", [L, D], F32)
        pos_t = sb("pos_t", [D, L], F32)
        pos_w = sb("pos_w", [D, L], F32)
        n_in, cinv = sb("n_in", [P, ST], F32), sb("cinv", [P, ST], F32)
        row_ss, row_n = sb("row_ss", [P, NBLK], F32), sb("row_n", [P, NBLK], F32)
        ss, root, rsc = sb("ss", [P, 2], F32), sb("root", [P, 2], F32), sb("rsc", [P, 2], F32)
        iota_q = sb("iota_q", [P, P], BF16)
        iota_t = sb("iota_t", [P, CAPMAX], BF16)
        iota_r = sb("iota_r", [P, R], F32)
        iota_tq = sb("iota_tq", [P, QT], F32)
        ident = sb("ident", [P, P], F32)
        below = sb("below", [P, P], F32)
        zero_b = sb("zero_b", [P, P], BF16)
        ones_f = sb("ones_f", [P, P], F32)

        def bank(name):
            return ctx.enter_context(nc.psum_tensor(name, [P, 512], F32))

        ps_idx, ps_val = bank("ps_idx"), bank("ps_val")
        ps_rank = [bank("ps_rank0"), bank("ps_rank1")]
        ps_app = [ctx.enter_context(nc.psum_tensor(f"ps_app{n}", [P, W, R], F32)) for n in range(2)]

        s_rows, s_cols, s_vals = sem("rows_in"), sem("cols_in"), sem("vals_in")
        s_const = sem("constants_made")
        s_cz = sem("constants_cleared")
        s_dve = sem("vector_step")
        s_oh = sem("bins_onehot")
        s_hist = sem("histogram_made")
        s_cum = sem("histogram_summed")
        s_binof = sem("bin_of_tile")
        s_row1 = sem("bin_row_turned")
        s_pick = sem("ranks_picked")
        s_pickf = sem("picks_summed")
        s_rank = sem("ranks_made")
        s_pd = sem("perm_onehots")
        s_pa = sem("perm_values")
        s_pm = sem("perm_matmuls")
        s_pz = sem("perm_banks_done")
        s_ev = sem("perm_banks_read")
        s_idx = sem("indices_in_ring")
        s_g = [sem(f"gathered{n}") for n in range(RING)]
        s_hot = sem("rows_onehot")
        s_mm = sem("tile_products")
        s_add = sem("halves_added")
        s_acc = sem("tiles_added")
        s_clear = sem("accumulator_clear")
        s_h1 = sem("layer1_done")
        s_h1w = sem("layer1_stored")
        s_emb = sem("embeddings_in")
        s_out = [sem(f"out_stored{n}") for n in range(2)]
        s_w, s_w2 = sem("weights_in"), sem("weights2_in")
        s_wt, s_wtc = sem("weights_turned"), sem("weights_copied")
        s_sorted = sem("edges_sorted")
        s_ids = sem("session_ids_in")
        s_total = sem("total_begun")
        s_feat = sem("features_in")
        s_comb = sem("combined_made")
        s_combw = sem("combined_stored")
        s_sel = sem("indices_selected")
        s_rss = sem("row_squares")
        s_rroot = sem("row_roots")
        s_scaled = sem("rows_scaled")
        s_turned = sem("rows_turned")
        s_norm = sem("rows_placed")
        s_sidx = sem("session_indices")
        s_seq = [[sem(f"seq{n}_{q}") for q in range(L // GL)] for n in range(2)]
        s_tr = sem("places_turned")
        s_seqt = sem("places_copied")
        s_m1 = sem("hidden_products")
        s_tanh = sem("hidden_made")
        s_gate = sem("gates_made")
        s_hsl = sem("places_added_to_mean")
        s_sel_l = sem("places_added_to_session")
        s_used = sem("places_used")
        s_hsn = sem("mean_made")
        s_ht = sem("mean_turned")
        s_htc = sem("mean_copied")
        s_z = sem("gate_products")
        s_bt = sem("gates_summed")
        s_sess = sem("session_made")
        s_sst = sem("session_turned")
        s_sstc = sem("session_copied")
        s_ss = sem("session_square")
        s_root = sem("session_root")
        s_rsc = sem("session_scale")
        s_sc = [sem(f"score_block{n}") for n in range(2)]
        s_scev = [sem(f"score_staged{n}") for n in range(2)]
        s_beta = sem("place_weights")
        s_hsum = sem("mean_summed")
        s_join = sem("sums_joined")
        s_rsteps = sem("scale_steps")
        s_free = sem("stage_free")
        s_staged = sem("stage_full")

        h1 = nc.dram_tensor("h1_rows", [NBLK * P, D], F32, kind="Internal").ap()
        comb = nc.dram_tensor("combined_rows", [NBLK * P, D], F32, kind="Internal").ap()
        ps_turn = [ps_idx, ps_val]
        ps_hid = ps_rank
        ps_beta = [ps_app[0][:, 2 * n, 0:L] for n in range(2)]
        ps_mean, ps_sess = ps_app[0][:, 3, 0:P], ps_app[0][:, 1, 0:P]
        ps_score = [ps_app[1][:, 2 * n:2 * n + 2, :].rearrange("p a b -> p (a b)") for n in range(2)]

        def wait(eng, s, value):
            if not isinstance(value, int) or value > 0:
                eng.wait_ge(s, value)

        def session_steps(eng, step):
            step(0, 0, False, None)
            step(1, 1, True, None)
            with eng.Fori(0, (ST - 2) // 2) as i:
                step(2 * i + 2, 0, True, (i, 0))
                step(2 * i + 3, 1, True, (i, 1))
            step(ST, 0, True, (ST // 2 - 1, 0))
            step(ST + 1, 1, False, (ST // 2 - 1, 1))

        def score_block(c, j):
            i, par = c
            n = OB * par + j
            return n % 2, OB * i + n // 2 + 1, j * OBW, min(OBW, N - j * OBW)

        def evacuate_scores(eng, mine, c, j):
            i, par = c
            b, n, at, w = score_block(c, j)
            if b != mine:
                return
            q, m = j // OG, OG * par + j // OG
            eng.wait_ge(s_sc[b], n)
            eng.wait_ge(s_rsc, 2 * i + par + 1)
            eng.wait_ge(s_free, 2 * OG * i + m + 1)
            dst = stage[:, m % 2, (j % OG) * OBW:(j % OG) * OBW + w]
            scale = rsc[:, par:par + 1]
            if mine:
                ins = eng.activation(dst, ps_score[b][:, 0:w], ACT.Copy, scale=scale)
            else:
                ins = eng.tensor_scalar(dst, ps_score[b][:, 0:w], scale, None, ALU.mult)
            ins.then_inc(s_scev[b], 1)

        halves = [c // W for c in CAPS]
        units = [c // PW for c in CHUNKS]
        phases = halves + [TILES // W]
        idx_base = [sum(phases[:n]) + RING * n for n in range(K + 2)]
        hot_base = [sum(phases[:n]) + 2 * n for n in range(K + 2)]
        mm_base = [sum(phases[:n]) for n in range(K + 2)]
        unit_base = [sum(units[:n]) for n in range(K + 1)]
        made_base = [b + AHEAD * n for n, b in enumerate(unit_base)]
        block = ctx.enter_context(nc.Block())

        def loop(eng, count, body, start=0):
            if count > start:
                with eng.Fori(start, count) as i:
                    body(i)

        def merged(eng, k, apply_turn, perm_turn):
            a = CAPS[k] // ROUND
            p = CHUNKS[k + 1] // PTURN if k + 1 < K else 0
            both = min(a, p)

            def two(i):
                for h in range(RING):
                    apply_turn(k, i, h)
                    perm_turn(k + 1, i, h)
            loop(eng, both, two)
            loop(eng, a, lambda i: [apply_turn(k, i, h) for h in range(RING)], both)
            loop(eng, p, lambda i: [perm_turn(k + 1, i, h) for h in range(RING)], both)

        @block.sync
        def _(sp):
            sp.dma_start(rows[0:EP, :], x["row"].rearrange("(p j) -> p j", p=EP)).then_inc(s_rows, 16)
            sp.dma_start(cols[0:EP, :], x["col"].rearrange("(p j) -> p j", p=EP)).then_inc(s_cols, 16)
            sp.dma_start(vals[0:EP, :], x["val"].rearrange("(p j) -> p j", p=EP)).then_inc(s_vals, 16)
            for t, src in ((w1a, x["w1"][0:P, :]), (w1b, x["w1"][P:2 * P, :]), (g1, x["g1"]), (g2, x["g2"]),
                           (pos, x["emb"][0:L, :]), (w2, x["w2"])):
                sp.dma_start(t[:], src).then_inc(s_w, 16)
            sp.dma_start(gb[:], x["gb"].rearrange("(p a) -> p a", a=1)).then_inc(s_w, 16)

            def load_table(dst, src, s):
                v = dst.rearrange("p (b d) -> p b d", d=D)
                sp.dma_start(v[:, 0:FULL, :], src[0:FULL * P, :].rearrange("(b p) d -> p b d", p=P)).then_inc(s, 16)
                sp.dma_start(v[0:LAST, FULL, :], src[FULL * P:N, :]).then_inc(s, 16)

            sp.wait_ge(s_sorted, 1)
            load_table(total, x["emb"], s_emb)
            for dst, src in ((items_i, "items"), (alias_i, "alias"), (inputs_i, "inputs")):
                sp.dma_start(dst, x[src].rearrange("(t p) l -> p t l", p=P)).then_inc(s_ids, 16)
            sp.wait_ge(s_h1, 1)
            sp.dma_start(h1.rearrange("(b p) d -> p b d", p=P),
                         acc.rearrange("p (b d) -> p b d", d=D)).then_inc(s_h1w, 16)
            sp.wait_ge(s_h1w, 16)
            sp.wait_ge(s_total, 1)
            load_table(acc, x["feat"], s_feat)
            comb_v = comb.rearrange("(b p) d -> p b d", p=P)
            for q in range(PIECES):
                w = NBLK // PIECES
                sp.wait_ge(s_comb, q + 1)
                sp.dma_start(comb_v[:, q * w:q * w + w, :],
                             acc[:, q * w * D:(q + 1) * w * D].rearrange("p (b d) -> p b d", d=D)).then_inc(s_combw, 16)

            sp.sem_inc(s_free, 2)

            def store_scores(c):
                i, par = c
                for q in range(OB // OG):
                    m = OG * par + q
                    j = q * OG + OG - 1
                    n = OB * par + j
                    sp.wait_ge(s_scev[0], OB * i + n // 2 + 2)
                    sp.sem_inc(s_staged, 1)
                    sp.wait_ge(s_scev[1], OB * i + (n + 1) // 2 + 1)
                    sp.sem_inc(s_staged, 1)
                    w = min(OG * OBW, N - q * OG * OBW)
                    sp.dma_start(out[bass.ds((2 * i + par) * P, P), q * OG * OBW:q * OG * OBW + w],
                                 stage[:, m % 2, 0:w]).then_inc(s_out[m % 2], 16)
                    sp.wait_ge(s_out[m % 2], 16 * (OG * i + m // 2 + 1))
                    sp.sem_inc(s_free, 1)
            with sp.Fori(0, ST // 2) as i:
                store_scores((i, 0))
                store_scores((i, 1))

        @block.gpsimd
        def _(pool):
            kw = dict(allow_small_or_imprecise_dtypes=True)
            pool.iota(iota_q[:], [[1, P]], base=0, channel_multiplier=0, **kw).then_inc(s_const, 1)
            pool.iota(iota_t[:], [[1, CAPMAX]], base=-MID, channel_multiplier=0, **kw).then_inc(s_const, 1)
            pool.iota(iota_r[:], [[1, R]], base=0, channel_multiplier=0, **kw).then_inc(s_const, 1)
            pool.iota(iota_tq[:], [[P, QT]], base=0, channel_multiplier=1, **kw).then_inc(s_const, 1)
            pool.memset(ones_f[:], 1.0).then_inc(s_cz, 1)
            pool.memset(zero_b[:], 0.0).then_inc(s_cz, 1)
            pool.memset(ident[:], 0.0).then_inc(s_cz, 1)
            pool.wait_ge(s_cz, 3)
            pool.affine_select(out=ident[:], in_=ident[:], compare_op=ALU.not_equal, fill=1.0,
                               base=0, pattern=[[-1, P]], channel_multiplier=1).then_inc(s_const, 1)
            pool.affine_select(out=below[:], in_=ones_f[:], compare_op=ALU.is_ge, fill=0.0,
                               base=-1, pattern=[[1, P]], channel_multiplier=-1).then_inc(s_const, 1)
            for k in range(K + 1):
                table = x["emb"] if k < K else h1
                if k == K:
                    pool.wait_ge(s_h1w, 16)

                def turn(i):
                    for h in range(RING):
                        pool.wait_ge(s_idx, idx_base[k] + i * RING + h + 1)
                        pool.sem_inc(s_cz, 1)
                        for u in range(W):
                            n = h * W + u
                            pool.indirect_dma_start(
                                out=gath[:, h, u, :], out_offset=None, in_=table[:, :],
                                in_offset=bass.IndirectOffsetOnAxis(ap=iring[:, n:n + 1], axis=0),
                            ).then_inc(s_g[h], 16)
                loop(pool, phases[k] // RING, turn)
            pool.wait_ge(s_combw, 16 * PIECES)
            with pool.Fori(0, ST // 2) as i:
                for par in range(2):
                    pool.wait_ge(s_sidx, 2 * i + par + 1)
                    pool.sem_inc(s_cz, 1)
                    for l in range(L):
                        if l % GL == 0:
                            pool.wait_ge(s_used, (2 * i + par) * (L // GL) + l // GL + 1)
                            pool.sem_inc(s_cz, 1)
                        pool.indirect_dma_start(
                            out=seq[par][:, l, :], out_offset=None, in_=comb[:, :],
                            in_offset=bass.IndirectOffsetOnAxis(ap=idx50[:, par, l:l + 1], axis=0),
                        ).then_inc(s_seq[par][l // GL], 16)

        CONSTS = 6

        @block.vector
        def _(dve):
            steps = [0]

            def link(ins):
                steps[0] = steps[0] + 1
                ins.then_inc(s_dve, 1)
                dve.wait_ge(s_dve, steps[0])

            def prep(k):
                c, at = CHUNKS[k], slice(COL0[k], COL0[k + 1])
                e = slice(0, EP)
                if k == 0:
                    dve.wait_ge(s_rows, 16)
                link(dve.tensor_scalar(t0[e, 0:c], rows[e, at], 8, None, ALU.arith_shift_right))
                dve.tensor_copy(binb[e, 0:c], t0[e, 0:c])
                link(dve.tensor_scalar(t1[e, 0:c], rows[e, at], R - 1, None, ALU.bitwise_and))
                if k == 0:
                    dve.wait_ge(s_cols, 16)
                link(dve.scalar_tensor_tensor(out=pk[e, 0:c], in0=t1[e, 0:c], scalar=float(1 << COLBITS),
                                              in1=cols[e, at], op0=ALU.mult, op1=ALU.add))
                link(dve.tensor_scalar(t0[e, 0:c], pk[e, 0:c], (1 << LO) - 1, None, ALU.bitwise_and))
                link(dve.tensor_scalar(t1[e, 0:c], pk[e, 0:c], LO, None, ALU.arith_shift_right))
                dve.tensor_scalar(lo[e, 0:c], t0[e, 0:c], 1.0 / 64, None, ALU.mult)
                dve.tensor_scalar(hi[e, 0:c], t1[e, 0:c], float(1 << LO) / 64, None, ALU.mult)
                if k == 0:
                    dve.wait_ge(s_vals, 16)
                link(dve.tensor_copy(vb[e, 0:c], vals[e, at]))
                dve.tensor_copy(v1[e, 0:c], vb[e, 0:c])
                link(dve.tensor_tensor(r1[e, 0:c], vals[e, at], vb[e, 0:c], ALU.subtract))
                link(dve.tensor_copy(vb[e, 0:c], r1[e, 0:c]))
                dve.tensor_copy(v2[e, 0:c], vb[e, 0:c])
                link(dve.tensor_tensor(v3[e, 0:c], r1[e, 0:c], vb[e, 0:c], ALU.subtract))

            def rank(k):
                c, e = CHUNKS[k], slice(0, EP)
                oh2, seen2 = (v[e, 0:NB * c].rearrange("p (b c) -> p b c", c=c) for v in (oh, seen))

                def onehot(i):
                    for u in range(BG):
                        dve.tensor_scalar(oh2[:, bass.ds(i * BG + u, 1), :].rearrange("p a c -> p (a c)"),
                                          binb[e, 0:c], iota_r[e, bass.ds(i * BG + u, 1)], None,
                                          ALU.is_equal).then_inc(s_oh, 1)
                loop(dve, NB // BG, onehot)
                dve.wait_ge(s_oh, (k + 1) * NB)
                link(dve.tensor_tensor_scan(seen[e, 0:NB * c], ones_f[e, 0:1].to_broadcast([EP, NB * c]),
                                            oh[e, 0:NB * c], 0.0, ALU.mult, ALU.add))
                link(dve.tensor_copy(upto[e, :].unsqueeze(2), seen2[:, :, c - 1:c]))
                dve.tensor_copy(hist[e, 0:1], upto[e, 0:1])
                link(dve.tensor_tensor(hist[e, 1:NB], upto[e, 1:NB], upto[e, 0:NB - 1], ALU.subtract))
                dve.sem_inc(s_hist, 1)
                link(dve.tensor_tensor(upto[e, :], hist[e, :], upto[e, :], ALU.subtract))
                dve.wait_ge(s_cum, k + 1)
                link(dve.tensor_scalar(tiles_i[:], ps_rank[1][:, 0:NB], float(P - 1), None, ALU.add))
                link(dve.tensor_scalar(tiles_i[:], tiles_i[:], 7, None, ALU.arith_shift_right))
                link(dve.tensor_copy(tiles_f[:], tiles_i[:]))
                link(dve.tensor_tensor_scan(tiles_inc[:], ones_f[:, 0:NB], tiles_f[:], 0.0, ALU.mult, ALU.add))
                link(dve.tensor_tensor(base[:], tiles_inc[:], tiles_f[:], ALU.subtract))
                link(dve.tensor_scalar(base[:], base[:], float(P), -1.0, ALU.mult, ALU.add))
                link(dve.tensor_tensor(base[e, :], base[e, :], ps_rank[1][e, NB:2 * NB], ALU.add))
                link(dve.tensor_tensor(base[e, :], base[e, :], upto[e, :], ALU.add))
                link(dve.tensor_tensor(past[:], iota_tq[:].unsqueeze(2).to_broadcast([P, QT, NB - 1]),
                                       tiles_inc[:, 0:NB - 1].unsqueeze(1).to_broadcast([P, QT, NB - 1]),
                                       ALU.is_ge))
                link(dve.tensor_reduce(bin_of[:], past[:], AX.X, ALU.add))
                dve.tensor_scalar(bin_of[:], bin_of[:], float(R), None, ALU.mult).then_inc(s_binof, 1)

                def pick(i):
                    for u in range(BG):
                        dve.wait_ge(s_pickf, k * NB + i * BG + u + 1)
                        b = bass.ds(i * BG + u, 1)
                        dve.scalar_tensor_tensor(out=picked[e, u, 0:c],
                                                 in0=seen2[:, b, :].rearrange("p a c -> p (a c)"), scalar=base[e, b],
                                                 in1=oh2[:, b, :].rearrange("p a c -> p (a c)"),
                                                 op0=ALU.add, op1=ALU.mult).then_inc(s_pick, 1)
                loop(dve, NB // BG, pick)
                dve.wait_ge(s_row1, k + 1)
                dve.tensor_copy(tab[0:1, TILE0[k]:TILE0[k + 1]], ps_rank[1][0:1, 0:CAPS[k]])
                dve.wait_ge(s_rank, k + 1)
                link(dve.tensor_copy(pk[e, 0:c], ps_rank[0][e, 0:c]))
                link(dve.tensor_scalar(t0[e, 0:c], pk[e, 0:c], 7, None, ALU.arith_shift_right))
                link(dve.tensor_scalar(t1[e, 0:c], pk[e, 0:c], P - 1, None, ALU.bitwise_and))
                dve.tensor_scalar(tf[e, 0:c], t0[e, 0:c], float(-MID), None, ALU.add)
                link(dve.tensor_copy(qf[e, 0:c], t1[e, 0:c]))

            def make_unit(at0, n, cap):
                e = slice(0, EP)
                for u in range(PW):
                    at = bass.ds(at0 + u, 1)
                    dve.tensor_scalar(ohq[e, n, u, :], iota_q[e, :], qf[e, at], None, ALU.is_equal)
                    dve.tensor_scalar(ohi[e, n, u, 0:P], iota_q[e, :], qf[e, at], lo[e, at],
                                      ALU.is_equal, ALU.mult)
                    ins = dve.tensor_scalar(oht[e, n, u, 0:cap], iota_t[e, 0:cap], tf[e, at], None,
                                            ALU.is_equal)
                ins.then_inc(s_pd, 1)

            def start_perm(k):
                for n in range(AHEAD):
                    make_unit(n * PW, n, CAPS[k])

            def perm_turn(k, i, h):
                dve.wait_ge(s_pm, unit_base[k] + i * RING + h + 1)
                make_unit(i * PTURN + (h + AHEAD) * PW, (h + AHEAD) % RING, CAPS[k])

            def evacuate(k):
                cap, at = CAPS[k], slice(TILE0[k], TILE0[k + 1])
                dve.wait_ge(s_pz, k + 1)
                dve.wait_ge(s_pd, made_base[k + 1])
                word = arena[:, word_at:word_at + cap].bitcast(I32)
                part = arena[:, part_at:part_at + cap].bitcast(I32)
                link(dve.tensor_scalar(word, ps_idx[:, 0:cap], 64.0, None, ALU.mult))
                link(dve.tensor_scalar(idx_s[:, at], word, (1 << COLBITS) - 1, None, ALU.bitwise_and))
                link(dve.tensor_scalar(part, word, COLBITS, None, ALU.arith_shift_right))
                link(dve.tensor_copy(row_s[:, at], part))
                link(dve.tensor_copy(val_s[:, at], ps_val[:, 0:cap]))
                dve.sem_inc(s_ev, 1)

            def fill(t, h):
                dve.tensor_copy(iring[:, h * W:h * W + W], idx_s[:, bass.ds(t, W)]).then_inc(s_idx, 1)

            def make_hot(t, n, u):
                at = bass.ds(t, 1)
                return dve.tensor_scalar(hot[:, n, u, :], iota_r[:], row_s[:, at], val_s[:, at],
                                         ALU.is_equal, ALU.mult)

            def start_apply(k):
                first = TILE0[k] if k < K else 0
                if k:
                    dve.wait_ge(s_idx, idx_base[k])
                    dve.wait_ge(s_hot, hot_base[k])
                for h in range(RING):
                    fill(first + h * W, h)
                for n in range(2):
                    for u in range(W):
                        ins = make_hot(first + n * W + u, n, u)
                    ins.then_inc(s_hot, 1)

            regs = [[dve.alloc_register(f"bin_{h}_{u}") for u in range(W)] for h in range(RING)]

            def apply_turn(k, i, h):
                n = h % 2
                first = TILE0[k] if k < K else 0
                t = i * ROUND + (first + h * W)
                done = mm_base[k] * W
                dve.load(regs[h], tab[0:1, bass.ds(t, W)])
                offs = [dve.snap(r, min_val=0, max_val=(NB - 1) * R) for r in regs[h]]
                dve.wait_ge(s_mm, mm_base[k] + i * RING + h + 1)
                fill(t + ROUND, h)
                for u in range(W):
                    part = target(k)[:, bass.ds(offs[u], R)]
                    dve.wait_ge(s_acc, 1 + done + i * ROUND + h * W + u)
                    ins = dve.tensor_tensor(part, part, ps_app[n][:, u, :], ALU.add)
                    ins.then_inc(s_acc, 1)
                    last = make_hot(t + 2 * W + u, n, u)
                last.then_inc(s_hot, 1)
                dve.wait_ge(s_acc, 1 + done + i * ROUND + h * W + W)
                dve.sem_inc(s_add, 1)

            def target(k):
                return acc if k < K else total

            for v in (lo, qf, tf):
                link(dve.memset(v[0:EP, :], 0.0))
            link(dve.memset(acc, 0.0))
            link(dve.memset(idx_s, 0))
            link(dve.memset(row_s, 0.0))
            link(dve.memset(val_s, 0.0))
            link(dve.memset(tab[:], 0))
            dve.sem_inc(s_acc, 1)
            dve.sem_inc(s_add, 2)
            dve.wait_ge(s_const, CONSTS)
            prep(0)
            rank(0)
            start_perm(0)
            loop(dve, CHUNKS[0] // PTURN, lambda i: [perm_turn(0, i, h) for h in range(RING)])
            evacuate(0)
            for k in range(K):
                start_apply(k)
                if k + 1 < K:
                    prep(k + 1)
                    rank(k + 1)
                    start_perm(k + 1)
                else:
                    link(dve.memset(total[:, FULL * D:NBLK * D], 0.0))
                    dve.sem_inc(s_sorted, 1)
                merged(dve, k, apply_turn, perm_turn)
                if k + 1 < K:
                    evacuate(k + 1)
            dve.sem_inc(s_h1, 1)
            dve.wait_ge(s_emb, 32)
            dve.tensor_tensor(total, total, acc, ALU.add).then_inc(s_total, 1)
            dve.wait_ge(s_ids, 48)
            link(dve.tensor_copy(items_f, items_i))
            link(dve.tensor_scalar(wrap, items_f, 0.0, float(N), ALU.is_lt, ALU.mult))
            link(dve.tensor_tensor(items_f, items_f, wrap, ALU.add))
            link(dve.tensor_scalar(items_f, items_f, 0.0, float(N - 1), ALU.max, ALU.min))
            link(dve.tensor_copy(alias_f, alias_i))
            link(dve.tensor_scalar(mask, inputs_i, 0.0, None, ALU.not_equal))
            link(dve.tensor_reduce(n_in[:], mask, AX.X, ALU.add))
            link(dve.reciprocal(cinv[:], n_in[:]))
            link(dve.memset(idx_f, 0.0))
            dve.wait_ge(s_total, 1)
            dve.sem_inc(s_sel, 1)
            start_apply(K)

            def select(i):
                dve.wait_ge(s_sel, ST * i + 1)
                for t in range(ST):
                    dve.scalar_tensor_tensor(out=scrap[:, t, :], in0=iota_r[:, 0:L], scalar=alias_f[:, t, bass.ds(i, 1)],
                                             in1=items_f[:, t, :], op0=ALU.is_equal, op1=ALU.mult,
                                             accum_out=idx_f[:, t, bass.ds(i, 1)]).then_inc(s_sel, 1)
            loop(dve, L, lambda i: [select(i), [apply_turn(K, i, h) for h in range(RING)]])
            loop(dve, phases[K] // RING, lambda i: [apply_turn(K, i, h) for h in range(RING)], L)

            dve.wait_ge(s_sel, 1 + ST * L)
            dve.wait_ge(s_feat, 32)
            w = NBLK // PIECES * D
            for q in range(PIECES):
                at = slice(q * w, q * w + w)
                dve.scalar_tensor_tensor(out=acc[:, at], in0=total[:, at], scalar=1.0 / 3, in1=acc[:, at],
                                         op0=ALU.mult, op1=ALU.add).then_inc(s_comb, 1)

            def fill_session(t, par):
                dve.tensor_copy(idx50[:, par, :], idx_f[:, t, :] if isinstance(t, int) else
                                idx_f[:, bass.ds(t, 1), :].rearrange("p a l -> p (a l)")).then_inc(s_sidx, 1)
            fill_session(0, 0)
            dve.wait_ge(s_combw, 16 * PIECES)
            fill_session(1, 1)
            dve.wait_ge(s_rroot, 1)
            link(dve.tensor_scalar(row_n[:], row_n[:], 1.0 / 3, EPS, ALU.mult, ALU.max))
            link(dve.reciprocal(row_n[:], row_n[:]))
            link(dve.tensor_scalar(row_n[:], row_n[:], 1.0 / 3, None, ALU.mult))
            total3 = total.rearrange("p (b d) -> p b d", d=D)

            def scale_rows(first, count, n, r):
                wait(dve, s_turned, r - 1)
                dve.tensor_tensor(turn_in[:, n, 0:count, :], total3[:, bass.ds(first, count), :],
                                  row_n[:, bass.ds(first, count)].unsqueeze(2).to_broadcast([P, count, D]),
                                  ALU.mult).then_inc(s_scaled, 1)
            scale_rows(0, SG, 0, 0)
            scale_rows(SG, SG, 1, 1)

            def scale_two(i):
                for n in range(2):
                    scale_rows(i * 2 * SG + n * SG, SG, n, 2 * i + n)
            loop(dve, TR // 2, scale_two, 1)
            scale_rows(TR * SG, NBLK - TR * SG, 0, TR)

            def add_places(sums, rows, weights, g, s, before):
                l0, wl = SGS[g]
                if g:
                    dve.wait_ge(s, before + g)
                for u in range(wl):
                    if g == 0:
                        ins = dve.tensor_scalar(sums[:, u, :], rows[:, u, :], weights(u), None, ALU.mult)
                    else:
                        ins = dve.scalar_tensor_tensor(out=sums[:, u, :], in0=rows[:, l0 + u, :],
                                                       scalar=weights(l0 + u), in1=sums[:, u, :],
                                                       op0=ALU.mult, op1=ALU.add)
                ins.then_inc(s, 1)

            def join(sums, s, before):
                dve.wait_ge(s, before + NG)
                h = SG // 2
                dve.tensor_tensor(sums[:, 0:h, :], sums[:, 0:h, :], sums[:, h:SG, :], ALU.add).then_inc(s_join, 1)

            def step(t, par, gated, c):
                first = not (isinstance(t, int) and t >= ST)

                def gather_side(g):
                    l0, wl = SGS[g]
                    n = (par * NG + g) % 2
                    dve.wait_ge(s_tr, t * NG + g + 1)
                    wait(dve, s_m1, t * NG + g - 1)
                    dve.tensor_copy(seq_t[:, n, 0:wl * P], ps_turn[n][:, 0:wl * P]).then_inc(s_seqt, 1)
                    add_places(hs, seq[par], lambda l: mask[:, bass.ds(t, 1), l], g, s_hsl, t * NG)

                def gate_side(g):
                    l0, wl = SGS[g]
                    dve.wait_ge(s_bt, (t - 1) * NG + g + 1)
                    at = slice(l0, l0 + wl)
                    dve.tensor_tensor(beta[:, at], ps_beta[g % 2][:, at],
                                      mask[:, bass.ds(t - 1, 1), at].rearrange("p a l -> p (a l)"),
                                      ALU.mult).then_inc(s_beta, 1)
                    dve.wait_ge(s_beta, (t - 1) * NG + g + 1)
                    add_places(sess, seq[1 - par], lambda l: beta[:, l:l + 1], g, s_sel_l, (t - 1) * NG)
                    for q in range(L // GL):
                        if l0 < (q + 1) * GL <= l0 + wl:
                            dve.wait_ge(s_sel_l, (t - 1) * NG + g + 1)
                            dve.sem_inc(s_used, 1)
                for g in range(NG):
                    if first:
                        gather_side(g)
                    if gated and g:
                        gate_side(g - 1)
                    if c:
                        for j in (2 * g, 2 * g + 1):
                            if j < OB:
                                evacuate_scores(dve, 0, c, j)
                if first:
                    join(hs, s_hsl, t * NG)
                    dve.wait_ge(s_join, t + max(0, t - 1) + 1 if isinstance(t, int) else 2 * t)
                    dve.tensor_tensor(hs[:, 0, :], hs[:, 0, :], hs[:, 1, :], ALU.add).then_inc(s_hsum, 1)
                    dve.wait_ge(s_hsum, t + 1)
                    wait(dve, s_ht, t)
                    dve.tensor_scalar(hs_n, hs[:, 0, :], cinv[:, bass.ds(t, 1)], None, ALU.mult).then_inc(s_hsn, 1)
                if gated:
                    gate_side(NG - 1)
                    join(sess, s_sel_l, (t - 1) * NG)
                    dve.wait_ge(s_join, min(t + 1, ST) + t if isinstance(t, int) else 2 * t + 1)
                    wait(dve, s_sst, t - 1)
                    dve.tensor_tensor(sess_n, sess[:, 0, :], sess[:, 1, :], ALU.add).then_inc(s_sess, 1)
                    dve.wait_ge(s_sess, t)
                    dve.scalar_tensor_tensor(out=sess_sq, in0=sess_n, scalar=1.0, in1=sess_n, op0=ALU.mult,
                                             op1=ALU.mult, accum_out=ss[:, 1 - par:2 - par]).then_inc(s_ss, 1)
                if first and not (isinstance(t, int) and t + 2 > ST):
                    fill_session(t + 2, par)
                if gated:
                    r = rsc[:, 1 - par:2 - par]
                    dve.wait_ge(s_root, t)
                    dve.tensor_scalar(r, root[:, 1 - par:2 - par], EPS, None, ALU.max).then_inc(s_rsteps, 1)
                    dve.wait_ge(s_rsteps, 2 * t - 1)
                    dve.reciprocal(r, r).then_inc(s_rsteps, 1)
                    dve.wait_ge(s_rsteps, 2 * t)
                    dve.tensor_scalar(r, r, W_K, None, ALU.mult).then_inc(s_rsc, 1)
            dve.sem_inc(s_used, 2 * (L // GL))
            dve.sem_inc(s_scev[0], 1)
            session_steps(dve, step)

        @block.tensor
        def _(pe):
            pe.wait_ge(s_const, CONSTS)
            pe.sem_inc(s_pm, RING - AHEAD)
            pe.sem_inc(s_pickf, BG)
            pe.wait_ge(s_w, 16 * 7)
            pe.transpose(ps_app[0][:, 0, 0:P], g1[:], ident[:])
            pe.transpose(ps_app[0][:, 0, P:2 * P], g2[:], ident[:])
            pe.transpose(ps_app[0][:, 1, 0:L], pos[:], ident[0:L, 0:L]).then_inc(s_wt, 1)
            pe.wait_ge(s_wtc, 3)
            pe.matmul(ps_app[0][:, 1, L:2 * L], w1a[:], pos_t[:], start=True, stop=True).then_inc(s_wt, 1)
            pe.wait_ge(s_wtc, 4)
            def rank(k):
                c, e = CHUNKS[k], slice(0, EP)
                pe.wait_ge(s_hist, k + 1)
                pe.matmul(ps_rank[1][:, 0:NB], ones_f[e, :], hist[e, :], start=True, stop=True)
                pe.matmul(ps_rank[1][:, NB:2 * NB], below[e, :], hist[e, :], start=True,
                          stop=True).then_inc(s_cum, 1)
                pe.wait_ge(s_binof, k + 1)
                for q in range(-(-CAPS[k] // P)):
                    w = min(P, CAPS[k] - q * P)
                    ins = pe.matmul(ps_rank[1][0:1, q * P:q * P + w], bin_of[:, q:q + 1], ident[:, 0:w],
                                    start=True, stop=True)
                ins.then_inc(s_row1, 1)
                dst = ps_rank[0][e, 0:c]
                pe.matmul(dst, zero_b[:, e], iota_t[:, 0:c], start=True, stop=False, skip_group_check=True)

                def add_picks(i):
                    for u in range(BG):
                        pe.wait_ge(s_pick, k * NB + i * BG + u + 1)
                        pe.matmul(dst, ident[e, e], picked[e, u, 0:c], start=False, stop=False,
                                  skip_group_check=True).then_inc(s_pickf, 1)
                loop(pe, NB // BG, add_picks)
                pe.matmul(dst, zero_b[:, e], iota_t[:, 0:c], start=False, stop=True,
                          skip_group_check=True).then_inc(s_rank, 1)

            def open_banks(k):
                if k:
                    pe.wait_ge(s_ev, k)
                for b in (ps_idx, ps_val):
                    pe.matmul(b[:, 0:CAPS[k]], zero_b[:, :], iota_t[:, 0:CAPS[k]], start=True, stop=False,
                              skip_group_check=True)

            def perm_turn(k, i, h):
                n, cap = h, CAPS[k]
                pe.wait_ge(s_pa, unit_base[k] + i * RING + h + 1)
                for u in range(PW):
                    o = oht[0:EP, n, u, 0:cap]
                    for m in range(2):
                        pe.matmul(ps_idx[:, 0:cap], ohi[0:EP, n, u, m * P:m * P + P], o,
                                  start=False, stop=False, skip_group_check=True)
                    for m in range(3):
                        ins = pe.matmul(ps_val[:, 0:cap], ohv[0:EP, n, u, m * P:m * P + P], o,
                                        start=False, stop=False, skip_group_check=True)
                ins.then_inc(s_pm, 1)

            def close_banks(k):
                for b in (ps_idx, ps_val):
                    ins = pe.matmul(b[:, 0:CAPS[k]], zero_b[:, :], iota_t[:, 0:CAPS[k]], start=False, stop=True,
                                    skip_group_check=True)
                ins.then_inc(s_pz, 1)

            def apply_turn(k, i, h):
                n = h % 2
                used = mm_base[k] // RING * 64
                pe.wait_ge(s_hot, hot_base[k] + i * RING + h + 1)
                pe.wait_ge(s_g[h], used + i * 64 + 64)
                pe.wait_ge(s_add, mm_base[k] + i * RING + h + 1)
                for u in range(W):
                    for r in range(R // P):
                        ins = pe.matmul(ps_app[n][:, u, r * P:r * P + P], hot[:, n, u, r * P:r * P + P],
                                        gath[:, h, u, :], start=True, stop=True)
                ins.then_inc(s_mm, 1)

            rank(0)
            open_banks(0)
            loop(pe, CHUNKS[0] // PTURN, lambda i: [perm_turn(0, i, h) for h in range(RING)])
            close_banks(0)
            for k in range(K):
                if k + 1 < K:
                    rank(k + 1)
                    open_banks(k + 1)
                merged(pe, k, apply_turn, perm_turn)
                if k + 1 < K:
                    close_banks(k + 1)
            loop(pe, phases[K] // RING, lambda i: [apply_turn(K, i, h) for h in range(RING)])

            def turn_rows(count, n, r):
                pe.wait_ge(s_scaled, r + 1)
                wait(pe, s_norm, r - 1)
                for b in range(count):
                    ins = pe.transpose(ps_turn[n][:, b * P:b * P + P], turn_in[:, n, b, :], ident[:])
                ins.then_inc(s_turned, 1)
            turn_rows(SG, 0, 0)
            turn_rows(SG, 1, 1)
            loop(pe, TR // 2, lambda i: [turn_rows(SG, n, 2 * i + n) for n in range(2)], 1)
            turn_rows(NBLK - TR * SG, 0, TR)
            pe.wait_ge(s_norm, TR + 1)

            def scores(c, j):
                i, par = c
                b, n, at, w = score_block(c, j)
                if j == 0:
                    pe.wait_ge(s_sstc, 2 * i + par + 1)
                pe.wait_ge(s_scev[b], n)
                pe.matmul(ps_score[b][:, 0:w], sess_t[:, par, :], total[:, at:at + w],
                          start=True, stop=True).then_inc(s_sc[b], 1)

            def step(t, par, gated, c):
                first = not (isinstance(t, int) and t >= ST)
                half = t // 2 if isinstance(t, int) else c[0] + 1

                def turn(g):
                    l0, wl = SGS[g]
                    n = (par * NG + g) % 2
                    wait(pe, s_seqt, t * NG + g - 1)
                    for l in range(l0, l0 + wl):
                        if l % GL == 0:
                            pe.wait_ge(s_seq[par][l // GL], (half + 1) * (16 * GL))
                        ins = pe.transpose(ps_turn[n][:, (l - l0) * P:(l - l0 + 1) * P], seq[par][:, l, :], ident[:])
                    ins.then_inc(s_tr, 1)

                def hidden(g):
                    l0, wl = SGS[g]
                    pe.wait_ge(s_seqt, t * NG + g + 1)
                    wait(pe, s_tanh, t * NG + g)
                    pe.matmul(ps_hid[1][:, 0:wl * P], w1b[:], seq_t[:, (par * NG + g) % 2, 0:wl * P],
                              start=True, stop=True).then_inc(s_m1, 1)

                def gate_input(g):
                    l0, wl = SGS[g]
                    pe.wait_ge(s_tanh, (t - 1) * NG + g + 1)
                    wait(pe, s_gate, (t - 1) * NG + g)
                    if g == 0:
                        pe.wait_ge(s_htc, t)
                    dst = ps_hid[0][:, 0:wl * P]
                    pe.matmul(dst, g1_t[:], nh[:, l0 * P:(l0 + wl) * P], start=True, stop=False)
                    pe.matmul(dst, g2_t[:], hs_t.unsqueeze(1).to_broadcast([P, wl, P]), start=False,
                              stop=True).then_inc(s_z, 1)

                def weigh(g):
                    l0, wl = SGS[g]
                    pe.wait_ge(s_gate, (t - 1) * NG + g + 1)
                    if g >= 2:
                        pe.wait_ge(s_beta, (t - 1) * NG + g - 1)
                    n = ((1 - par) * NG + g) % 2
                    for l in range(l0, l0 + wl):
                        ins = pe.matmul(ps_beta[g % 2][:, l:l + 1], gate[:, n, (l - l0) * P:(l - l0 + 1) * P], w2[:],
                                        start=True, stop=True)
                    ins.then_inc(s_bt, 1)
                for g in range(NG):
                    if first:
                        turn(g)
                    if gated:
                        gate_input(g)
                    if first and g:
                        hidden(g - 1)
                    if gated and g:
                        weigh(g - 1)
                    if c:
                        for j in (2 * g, 2 * g + 1):
                            if j < OB:
                                scores(c, j)
                if first:
                    hidden(NG - 1)
                if gated:
                    weigh(NG - 1)
                if first:
                    pe.wait_ge(s_hsn, t + 1)
                    pe.transpose(ps_mean, hs_n, ident[:]).then_inc(s_ht, 1)
                if gated:
                    pe.wait_ge(s_sess, t)
                    pe.transpose(ps_sess, sess_n, ident[:]).then_inc(s_sst, 1)
            session_steps(pe, step)

        @block.scalar
        def _(act):
            def perm_turn(k, i, h):
                n, e = h, slice(0, EP)
                act.wait_ge(s_pd, made_base[k] + i * RING + h + 1)
                for u in range(PW):
                    at = bass.ds(i * PTURN + h * PW + u, 1)
                    act.activation(ohi[e, n, u, P:2 * P], ohq[e, n, u, :], ACT.Copy, scale=hi[e, at])
                    for m, v in enumerate((v1, v2, v3)):
                        ins = act.activation(ohv[e, n, u, m * P:m * P + P], ohq[e, n, u, :], ACT.Copy,
                                             scale=v[e, at])
                ins.then_inc(s_pa, 1)

            act.wait_ge(s_wt, 1)
            act.activation(g1_t[:], ps_app[0][:, 0, 0:P], ACT.Copy).then_inc(s_wtc, 1)
            act.activation(g2_t[:], ps_app[0][:, 0, P:2 * P], ACT.Copy).then_inc(s_wtc, 1)
            act.activation(pos_t[:], ps_app[0][:, 1, 0:L], ACT.Copy).then_inc(s_wtc, 1)
            act.wait_ge(s_wt, 2)
            act.activation(pos_w[:], ps_app[0][:, 1, L:2 * L], ACT.Copy).then_inc(s_wtc, 1)
            for k in range(K):
                loop(act, CHUNKS[k] // PTURN, lambda i: [perm_turn(k, i, h) for h in range(RING)])

            act.wait_ge(s_comb, PIECES)
            total3 = total.rearrange("p (b d) -> p b d", d=D)
            act.sem_inc(s_rss, 1)

            def squares(i):
                act.wait_ge(s_rss, i + 1)
                act.activation(square, total3[:, bass.ds(i, 1), :].rearrange("p a d -> p (a d)"), ACT.Square,
                               accum_out=row_ss[:, bass.ds(i, 1)]).then_inc(s_rss, 1)
            loop(act, NBLK, squares)
            act.wait_ge(s_rss, NBLK + 1)
            act.activation(row_n[:], row_ss[:], ACT.Sqrt).then_inc(s_rroot, 1)

            def place(first, count, n, r):
                act.wait_ge(s_turned, r + 1)
                act.activation(total[:, bass.ds(first * P, count * P)], ps_turn[n][:, 0:count * P],
                               ACT.Copy).then_inc(s_norm, 1)
            loop(act, TR // 2, lambda i: [place(i * 2 * SG + n * SG, SG, n, 2 * i + n) for n in range(2)])
            place(TR * SG, NBLK - TR * SG, 0, TR)

            def step(t, par, gated, c):
                first = not (isinstance(t, int) and t >= ST)

                def hidden(g):
                    l0, wl = SGS[g]
                    act.wait_ge(s_m1, t * NG + g + 1)
                    for l in range(l0, l0 + wl):
                        ins = act.activation(nh[:, l * P:l * P + P], ps_hid[1][:, (l - l0) * P:(l - l0 + 1) * P],
                                             ACT.Tanh, bias=pos_w[:, L - 1 - l:L - l])
                    ins.then_inc(s_tanh, 1)

                def gates(g):
                    l0, wl = SGS[g]
                    act.wait_ge(s_z, (t - 1) * NG + g + 1)
                    wait(act, s_bt, (t - 1) * NG + g - 1)
                    act.activation(gate[:, ((1 - par) * NG + g) % 2, 0:wl * P], ps_hid[0][:, 0:wl * P],
                                   ACT.Sigmoid, bias=gb[:]).then_inc(s_gate, 1)
                for g in range(NG):
                    if gated:
                        gates(g)
                    if first and g:
                        hidden(g - 1)
                    if c:
                        for j in (2 * g, 2 * g + 1):
                            if j < OB:
                                evacuate_scores(act, 1, c, j)
                if first:
                    hidden(NG - 1)
                    act.wait_ge(s_ht, t + 1)
                    act.activation(hs_t, ps_mean, ACT.Copy).then_inc(s_htc, 1)
                if gated:
                    act.wait_ge(s_sst, t)
                    act.activation(sess_t[:, 1 - par, :], ps_sess, ACT.Copy).then_inc(s_sstc, 1)
                    act.wait_ge(s_ss, t)
                    act.activation(root[:, 1 - par:2 - par], ss[:, 1 - par:2 - par], ACT.Sqrt).then_inc(s_root, 1)
            act.sem_inc(s_scev[1], 1)
            session_steps(act, step)


_INS = {"items": "r_items", "inputs": "r_inputs", "alias": "r_alias_inputs", "feat": "L0_rec_item_features",
        "row": "L0_rec_adj_row", "col": "L0_rec_adj_col", "val": "L0_rec_adj_val", "emb": "L0_rec_emb",
        "w1": "L0_rec_w_1", "w2": "L0_rec_w_2", "g1": "L0_rec_glu1_w", "gb": "L0_rec_glu1_b", "g2": "L0_rec_glu2_w"}


def kernel(**inputs):
    import concourse.bacc as bacc
    from concourse.bass_utils import run_bass_kernel_spmd

    nc = bacc.Bacc("TRN2", target_bir_lowering=False, num_devices=1)
    arrays, x = {}, {}
    for name, full in _INS.items():
        a = np.ascontiguousarray(inputs[full])
        arrays[f"in_{name}"] = a
        x[name] = nc.dram_tensor(f"in_{name}", a.shape, mybir.dt.from_np(a.dtype), kind="ExternalInput").ap()
    out = nc.dram_tensor("scores", (B, N), F32, kind="ExternalOutput").ap()
    build(nc, x, out)
    r = run_bass_kernel_spmd(nc, [arrays], core_ids=[0])
    return r.results[0]["scores"]
```

```python
from contextlib import ExitStack

import numpy as np

import concourse.bass as bass
from concourse import mybir

F32 = mybir.dt.float32
BF16 = mybir.dt.bfloat16
F16 = mybir.dt.float16
I32 = mybir.dt.int32
ALU = mybir.AluOpType
ACT = mybir.ActivationFunctionType
AX = mybir.AxisListType

P = 128
N, D = 12501, 128
E = 150000
EP = 125
EC = E // EP
R = 256
NB = -(-N // R)
NBLK = NB * R // P
FULL, LAST = N // P, N % P
BG = 7
CHUNKS = [256, 304, 320, 320]
assert sum(CHUNKS) == EC and NB % BG == 0
W = 4
RING = 4
PW = 4
PR = 4
AHEAD = 3
ROUND = W * RING
PTURN = PW * PR
CAPS = [-(-((EP * c + NB * (P - 1)) // P) // ROUND) * ROUND for c in CHUNKS]
CMAX, CAPMAX = max(CHUNKS), max(CAPS)
TILES = sum(CAPS)
TPAD = TILES + ROUND
TILE0 = [sum(CAPS[:k]) for k in range(len(CAPS) + 1)]
COL0 = [sum(CHUNKS[:k]) for k in range(len(CHUNKS) + 1)]
K = len(CHUNKS)
MID = CAPMAX // 2
LO = 11
COLBITS = 14
QT = -(-CAPMAX // P)
B, L = 1024, 50
ST = B // P
OBW = 512
OB = -(-N // OBW)
OG = 5
SG = 4
SGS = [(l, min(SG, L - l)) for l in range(0, L, SG)]
NG = len(SGS)
GL = 10
PIECES = 7
TR = NBLK // SG
RB = 7
RA = 10 * RB
W_K, EPS = 12.0, 1e-12
assert (NBLK - RA) % RB == 0
assert OB <= 2 * NG and OB == 5 * OG and NBLK % PIECES == 0 and ST % 2 == 0


def build(nc, x, out):
    ctx = ExitStack()
    with ctx:
        def sb(name, shape, dt):
            return ctx.enter_context(nc.sbuf_tensor(name, shape, dt))

        def sem(name):
            return ctx.enter_context(nc.semaphore(name))

        WORDS = 48640
        arena = sb("arena", [P, WORDS], F32)
        top = [0]

        def view(words, shape, dt, at=None, parts=P):
            start = top[0] if at is None else at
            if at is None:
                top[0] += words
            assert start + words <= WORDS, (start, words)
            v = arena[0:parts, start:start + words]
            if dt is not F32:
                v = v.bitcast(dt)
            names = " ".join("abcd"[:len(shape)])
            sizes = {"abcd"[n]: s for n, s in enumerate(shape)}
            if len(shape) > 1:
                v = v.rearrange(f"p ({names}) -> p {names}", **sizes)
            return v

        ACCW = NBLK * D
        acc = view(ACCW, [ACCW], F32)[:, 0:NBLK * D]
        low = top[0]
        rows = view(EC, [EC], I32)
        cols = view(EC, [EC], I32)
        vals = view(EC, [EC], F32)
        CPAD = CMAX + AHEAD * PW
        lo, hi, v1, v2, v3, qf, tf, t0, t1, pk = (view(CPAD, [CPAD], F32 if n < 7 else I32) for n in range(10))
        r1 = view(CMAX, [CMAX], F32)
        binb = view(CMAX // 2, [CMAX], BF16)
        vb = view(CMAX // 2, [CMAX], BF16)
        oh = view(CMAX * NB // 2, [NB * CMAX], BF16)
        cnt_at = top[0]
        seen = view(CMAX * NB // 2, [NB * CMAX], F16, at=cnt_at)
        picked = view(BG * CMAX, [BG, CMAX], F32, at=cnt_at + CMAX * NB // 2)
        oht = view(PR * PW * CAPMAX // 2, [PR, PW, CAPMAX], BF16)
        ohq = view(PR * PW * P // 2, [PR, PW, P], BF16)
        ohi = view(PR * PW * 2 * P // 2, [PR, PW, 2 * P], F16)
        ohv = view(PR * PW * 3 * P // 2, [PR, PW, 3 * P], BF16)
        word_at, part_at = cnt_at, cnt_at + CAPMAX
        top[0] = max(top[0], cnt_at + CMAX * NB // 2 + BG * CMAX)
        high = top[0] = max(top[0], low + ACCW + 2 * L * P + (2 * ST + 2) * L)
        idx_s = view(TPAD, [TPAD], I32)
        row_s = view(TPAD, [TPAD], F32)
        val_s = view(TPAD, [TPAD], F32)
        gath = view(RING * W * D, [RING, W, D], F32)
        hot = view(2 * W * R, [2, W, R], F32)

        total = view(ACCW, [ACCW], F32, at=low)
        seq = [view(L * D, [L, D], F32, at=a) for a in (0, low + ACCW)]
        stage = view(2 * OG * OBW, [2, OG * OBW], F32, at=L * D)
        nh_at = low + ACCW + L * D
        nh = view(L * P, [L * P], F32, at=nh_at)
        items_i, alias_i, inputs_i = (view(ST * L, [ST, L], I32, at=nh_at + n * ST * L) for n in range(3))
        wrap, items_f, alias_f, scrap = (view(ST * L, [ST, L], F32, at=nh_at + n * ST * L) for n in range(3, 7))
        top[0] = nh_at + L * P
        mask = view(ST * L, [ST, L], F32)
        idx_f = view((ST + 2) * L, [ST + 2, L], F32)
        assert top[0] <= high
        top[0] = high
        seq_t = view(2 * SG * P, [2, SG * P], F32)
        gate = view(2 * SG * P, [2, SG * P], F32)
        turn_in = view(2 * SG * P, [2, SG, P], F32)
        square = view(2 * RB * D, [2, RB, D], F32)
        hs = view(SG * D, [SG, D], F32)
        hs_n = view(D, [D], F32)
        hs_t = view(P, [P], F32)
        hs_w = view(P, [P], F32)
        sess = view(SG * D, [SG, D], F32)
        sess_n = view(D, [D], F32)
        sess_t = view(2 * P, [2, P], F32)
        sess_sq = view(D, [D], F32)
        beta = view(L, [L], F32)

        tiles_i = sb("tiles_i", [P, NB], I32)
        tiles_f = sb("tiles_f", [P, NB], F32)
        tiles_inc = sb("tiles_inc", [P, NB], F32)
        base = sb("base", [P, NB], F32)
        upto = sb("upto", [P, NB], F32)
        hist = sb("hist", [P, NB], F32)
        past = sb("past", [P, QT, NB - 1], F32)
        bin_of = sb("bin_of", [P, QT], F32)
        tab = sb("tab", [1, TPAD], I32)
        iring = sb("iring", [P, RING * W], I32)
        idx50 = sb("idx50", [P, 2, L], I32)
        w1a, w1b, g1, g2, g1_t, g2_t = (sb(n, [P, P], F32) for n in ("w1a", "w1b", "g1", "g2", "g1_t", "g2_t"))
        w2, gb = sb("w2", [P, 1], F32), sb("gb", [P, 1], F32)
        pos = sb("pos", [L, D], F32)
        pos_t = sb("pos_t", [D, L], F32)
        pos_w = sb("pos_w", [D, L], F32)
        n_in, cinv = sb("n_in", [P, ST], F32), sb("cinv", [P, ST], F32)
        row_ss, row_n = sb("row_ss", [P, NBLK], F32), sb("row_n", [P, NBLK], F32)
        ss, root, rsc = sb("ss", [P, 2], F32), sb("root", [P, 2], F32), sb("rsc", [P, 2], F32)
        iota_q = sb("iota_q", [P, P], BF16)
        iota_t = sb("iota_t", [P, CAPMAX], BF16)
        iota_r = sb("iota_r", [P, R], F32)
        iota_tq = sb("iota_tq", [P, QT], F32)
        ident = sb("ident", [P, P], F32)
        below = sb("below", [P, P], F32)
        zero_b = sb("zero_b", [P, P], BF16)
        ones_f = sb("ones_f", [P, P], F32)

        def bank(name):
            return ctx.enter_context(nc.psum_tensor(name, [P, 512], F32))

        ps_idx, ps_val = bank("ps_idx"), bank("ps_val")
        ps_rank = [bank("ps_rank0"), bank("ps_rank1")]
        ps_app = [ctx.enter_context(nc.psum_tensor(f"ps_app{n}", [P, W, R], F32)) for n in range(2)]

        s_rows, s_cols, s_vals = sem("rows_in"), sem("cols_in"), sem("vals_in")
        s_const = sem("constants_made")
        s_cz = sem("constants_cleared")
        s_dve = sem("vector_step")
        s_oh = sem("bins_onehot")
        s_hist = sem("histogram_made")
        s_cum = sem("histogram_summed")
        s_binof = sem("bin_of_tile")
        s_row1 = sem("bin_row_turned")
        s_pick = sem("ranks_picked")
        s_pickf = sem("picks_summed")
        s_rank = sem("ranks_made")
        s_q = sem("places_onehot")
        s_pd = sem("perm_onehots")
        s_pa = sem("perm_values")
        s_pp = sem("perm_values_pool")
        s_pm = sem("perm_matmuls")
        s_pz = sem("perm_banks_done")
        s_ev = sem("perm_banks_read")
        s_idx = sem("indices_in_ring")
        s_g = [sem(f"gathered{n}") for n in range(RING)]
        s_hot = sem("rows_onehot")
        s_mm = sem("tile_products")
        s_add = sem("halves_added")
        s_acc = sem("tiles_added")
        s_clear = sem("accumulator_clear")
        s_h1 = sem("layer1_done")
        s_h1w = sem("layer1_stored")
        s_emb = sem("embeddings_in")
        s_out = [sem(f"out_stored{n}") for n in range(2)]
        s_w, s_w2 = sem("weights_in"), sem("weights2_in")
        s_wt, s_wtc = sem("weights_turned"), sem("weights_copied")
        s_sorted = sem("edges_sorted")
        s_ids = sem("session_ids_in")
        s_total = sem("total_begun")
        s_feat = sem("features_in")
        s_l2 = sem("layer2_done")
        s_comb = sem("combined_made")
        s_combw = sem("combined_stored")
        s_sel = sem("indices_selected")
        s_rss = [sem("row_squares_scalar"), sem("row_squares_vector")]
        s_rroot = sem("row_roots")
        s_scaled = sem("rows_scaled")
        s_turned = sem("rows_turned")
        s_norm = sem("rows_placed")
        s_sidx = sem("session_indices")
        s_seq = [[sem(f"seq{n}_{q}") for q in range(L // GL)] for n in range(2)]
        s_tr = sem("places_turned")
        s_seqt = sem("places_copied")
        s_m1 = sem("hidden_products")
        s_tanh = sem("hidden_made")
        s_gate = sem("gates_made")
        s_hsl = sem("places_added_to_mean")
        s_sel_l = sem("places_added_to_session")
        s_used = sem("places_used")
        s_hsn = sem("mean_made")
        s_ht = sem("mean_turned")
        s_htc = sem("mean_copied")
        s_hw = sem("mean_products")
        s_hwc = sem("mean_products_copied")
        s_z = sem("gate_products")
        s_zin = sem("gate_inputs")
        s_bt = sem("gates_summed")
        s_sess = sem("session_made")
        s_sst = sem("session_turned")
        s_sstc = sem("session_copied")
        s_ss = sem("session_square")
        s_root = sem("session_root")
        s_rsc = sem("session_scale")
        s_sc = [sem(f"score_block{n}") for n in range(2)]
        s_scev = [sem(f"score_staged{n}") for n in range(2)]
        s_beta = sem("place_weights")
        s_hsum = sem("mean_summed")
        s_join = sem("sums_joined")
        s_rsteps = sem("scale_steps")
        s_free = sem("stage_free")
        s_staged = sem("stage_full")

        h1 = nc.dram_tensor("h1_rows", [NBLK * P, D], F32, kind="Internal").ap()
        comb = nc.dram_tensor("combined_rows", [NBLK * P, D], F32, kind="Internal").ap()
        ps_turn = [ps_idx, ps_val]
        ps_hid = ps_rank
        ps_beta = [ps_app[0][:, 2 * n, 0:L] for n in range(2)]
        ps_hw = ps_app[0][:, 3, P:2 * P]
        ps_mean, ps_sess = ps_app[0][:, 3, 0:P], ps_app[0][:, 1, 0:P]
        ps_score = [ps_app[1][:, 2 * n:2 * n + 2, :].rearrange("p a b -> p (a b)") for n in range(2)]

        def wait(eng, s, value):
            if not isinstance(value, int) or value > 0:
                eng.wait_ge(s, value)

        def session_steps(eng, step):
            step(0, 0, False, None)
            step(1, 1, True, None)
            with eng.Fori(0, (ST - 2) // 2) as i:
                step(2 * i + 2, 0, True, (i, 0))
                step(2 * i + 3, 1, True, (i, 1))
            step(ST, 0, True, (ST // 2 - 1, 0))
            step(ST + 1, 1, False, (ST // 2 - 1, 1))

        def score_blocks(g):
            return range(max(0, 2 * g - 2), min(2 * g, OB))

        def score_block(c, j):
            i, par = c
            n = OB * par + j
            return n % 2, OB * i + n // 2 + 1, j * OBW, min(OBW, N - j * OBW)

        def evacuate_scores(eng, mine, c, j):
            i, par = c
            b, n, at, w = score_block(c, j)
            if b != mine:
                return
            q, m = j // OG, OG * par + j // OG
            eng.wait_ge(s_sc[b], n)
            eng.wait_ge(s_rsc, 2 * i + par + 1)
            eng.wait_ge(s_free, 2 * OG * i + m + 1)
            dst = stage[:, m % 2, (j % OG) * OBW:(j % OG) * OBW + w]
            scale = rsc[:, par:par + 1]
            if mine:
                ins = eng.activation(dst, ps_score[b][:, 0:w], ACT.Copy, scale=scale)
            else:
                ins = eng.tensor_scalar(dst, ps_score[b][:, 0:w], scale, None, ALU.mult)
            ins.then_inc(s_scev[b], 1)

        halves = [c // W for c in CAPS]
        units = [c // PW for c in CHUNKS]
        phases = halves + [TILES // W]
        idx_base = [sum(phases[:n]) + RING * n for n in range(K + 2)]
        hot_base = [sum(phases[:n]) + 2 * n for n in range(K + 2)]
        mm_base = [sum(phases[:n]) for n in range(K + 2)]
        unit_base = [sum(units[:n]) for n in range(K + 1)]
        made_base = [b + AHEAD * n for n, b in enumerate(unit_base)]
        block = ctx.enter_context(nc.Block())

        def loop(eng, count, body, start=0):
            if count > start:
                with eng.Fori(start, count) as i:
                    body(i)

        def merged(eng, k, apply_turn, perm_turn):
            a = CAPS[k] // ROUND
            p = CHUNKS[k + 1] // PTURN if k + 1 < K else 0
            both = min(a, p)

            def two(i):
                for h in range(RING):
                    apply_turn(k, i, h)
                    if h < PR:
                        perm_turn(k + 1, i, h)
            loop(eng, both, two)
            loop(eng, a, lambda i: [apply_turn(k, i, h) for h in range(RING)], both)
            loop(eng, p, lambda i: [perm_turn(k + 1, i, h) for h in range(PR)], both)

        @block.sync
        def _(sp):
            sp.dma_start(rows[0:EP, :], x["row"].rearrange("(p j) -> p j", p=EP)).then_inc(s_rows, 16)
            sp.dma_start(cols[0:EP, :], x["col"].rearrange("(p j) -> p j", p=EP)).then_inc(s_cols, 16)
            sp.dma_start(vals[0:EP, :], x["val"].rearrange("(p j) -> p j", p=EP)).then_inc(s_vals, 16)
            for t, src in ((w1a, x["w1"][0:P, :]), (w1b, x["w1"][P:2 * P, :]), (g1, x["g1"]), (g2, x["g2"]),
                           (pos, x["emb"][0:L, :]), (w2, x["w2"])):
                sp.dma_start(t[:], src).then_inc(s_w, 16)
            sp.dma_start(gb[:], x["gb"].rearrange("(p a) -> p a", a=1)).then_inc(s_w, 16)

            def load_table(dst, src, s, k):
                v = dst.rearrange("p (b d) -> p b d", d=D)
                w = NBLK // PIECES
                for q in range(PIECES):
                    b = slice(q * w, min(q * w + w, FULL))
                    sp.wait_ge(s_mm, mm_base[k] + RING * q + 1)
                    sp.dma_start(v[:, b, :], src[b.start * P:b.stop * P, :].rearrange("(b p) d -> p b d",
                                                                                      p=P)).then_inc(s, 16)
                sp.dma_start(v[0:LAST, FULL, :], src[FULL * P:N, :]).then_inc(s, 16)

            sp.wait_ge(s_sorted, 1)
            load_table(total, x["emb"], s_emb, K - 1)
            for dst, src in ((items_i, "items"), (alias_i, "alias"), (inputs_i, "inputs")):
                sp.dma_start(dst, x[src].rearrange("(t p) l -> p t l", p=P)).then_inc(s_ids, 16)
            sp.wait_ge(s_h1, 1)
            sp.dma_start(h1.rearrange("(b p) d -> p b d", p=P),
                         acc.rearrange("p (b d) -> p b d", d=D)).then_inc(s_h1w, 16)
            sp.wait_ge(s_h1w, 16)
            sp.wait_ge(s_total, 1)
            load_table(acc, x["feat"], s_feat, K)
            comb_v = comb.rearrange("(b p) d -> p b d", p=P)
            for q in range(PIECES):
                w = NBLK // PIECES
                sp.wait_ge(s_comb, q + 1)
                sp.dma_start(comb_v[:, q * w:q * w + w, :],
                             acc[:, q * w * D:(q + 1) * w * D].rearrange("p (b d) -> p b d", d=D)).then_inc(s_combw, 16)

            sp.sem_inc(s_free, 2)

            def store_scores(c):
                i, par = c
                for q in range(OB // OG):
                    m = OG * par + q
                    j = q * OG + OG - 1
                    n = OB * par + j
                    sp.wait_ge(s_scev[0], OB * i + n // 2 + 2)
                    sp.sem_inc(s_staged, 1)
                    sp.wait_ge(s_scev[1], OB * i + (n + 1) // 2 + 1)
                    sp.sem_inc(s_staged, 1)
                    w = min(OG * OBW, N - q * OG * OBW)
                    sp.dma_start(out[bass.ds((2 * i + par) * P, P), q * OG * OBW:q * OG * OBW + w],
                                 stage[:, m % 2, 0:w]).then_inc(s_out[m % 2], 16)
                    sp.wait_ge(s_out[m % 2], 16 * (OG * i + m // 2 + 1))
                    sp.sem_inc(s_free, 1)
            with sp.Fori(0, ST // 2) as i:
                store_scores((i, 0))
                store_scores((i, 1))

        @block.gpsimd
        def _(pool):
            kw = dict(allow_small_or_imprecise_dtypes=True)
            pool.iota(iota_q[:], [[1, P]], base=0, channel_multiplier=0, **kw).then_inc(s_const, 1)
            pool.iota(iota_t[:], [[1, CAPMAX]], base=-MID, channel_multiplier=0, **kw).then_inc(s_const, 1)
            pool.iota(iota_r[:], [[1, R]], base=0, channel_multiplier=0, **kw).then_inc(s_const, 1)
            pool.iota(iota_tq[:], [[P, QT]], base=0, channel_multiplier=1, **kw).then_inc(s_const, 1)
            pool.memset(ones_f[:], 1.0).then_inc(s_cz, 1)
            pool.memset(zero_b[:], 0.0).then_inc(s_cz, 1)
            pool.memset(ident[:], 0.0).then_inc(s_cz, 1)
            pool.wait_ge(s_cz, 3)
            pool.affine_select(out=ident[:], in_=ident[:], compare_op=ALU.not_equal, fill=1.0,
                               base=0, pattern=[[-1, P]], channel_multiplier=1).then_inc(s_const, 1)
            pool.affine_select(out=below[:], in_=ones_f[:], compare_op=ALU.is_ge, fill=0.0,
                               base=-1, pattern=[[1, P]], channel_multiplier=-1).then_inc(s_const, 1)
            for v in (lo, hi, v1, qf, tf):
                pool.memset(v[0:EP, :], 0.0).then_inc(s_const, 1)
            pool.memset(tab[:], 0).then_inc(s_const, 1)
            for v in (idx_s, row_s, val_s, acc):
                pool.memset(v, 0.0 if v is not idx_s else 0).then_inc(s_clear, 1)

            def perm_turn(i, h):
                e, at = slice(0, EP), bass.ds(i * PTURN + h * PW, PW)
                pool.wait_ge(s_pd, i * PR + h + 1)
                for dst, v in ((ohi[e, h, :, P:2 * P], hi), (ohv[e, h, :, 0:P], v1)):
                    pool.tensor_tensor(dst, ohq[e, h], v[e, at].unsqueeze(2).to_broadcast([EP, PW, P]),
                                       ALU.mult).then_inc(s_pp, 1)
            loop(pool, CHUNKS[0] // PTURN, lambda i: [perm_turn(i, h) for h in range(PR)])
            for k in range(K + 1):
                table = x["emb"] if k < K else h1
                if k == K:
                    pool.wait_ge(s_h1w, 16)

                def turn(i):
                    for h in range(RING):
                        pool.wait_ge(s_idx, idx_base[k] + i * RING + h + 1)
                        pool.sem_inc(s_cz, 1)
                        for u in range(W):
                            n = h * W + u
                            pool.indirect_dma_start(
                                out=gath[:, h, u, :], out_offset=None, in_=table[:, :],
                                in_offset=bass.IndirectOffsetOnAxis(ap=iring[:, n:n + 1], axis=0),
                            ).then_inc(s_g[h], 16)
                loop(pool, phases[k] // RING, turn)
            pool.wait_ge(s_combw, 16 * PIECES)
            with pool.Fori(0, ST // 2) as i:
                for par in range(2):
                    pool.wait_ge(s_sidx, 2 * i + par + 1)
                    pool.sem_inc(s_cz, 1)
                    for l in range(L):
                        if l % GL == 0:
                            pool.wait_ge(s_used, (2 * i + par) * (L // GL) + l // GL + 1)
                            pool.sem_inc(s_cz, 1)
                        pool.indirect_dma_start(
                            out=seq[par][:, l, :], out_offset=None, in_=comb[:, :],
                            in_offset=bass.IndirectOffsetOnAxis(ap=idx50[:, par, l:l + 1], axis=0),
                        ).then_inc(s_seq[par][l // GL], 16)

        CONSTS, CLEARED = 12, 4

        @block.vector
        def _(dve):
            steps = [0]

            def link(ins):
                steps[0] = steps[0] + 1
                ins.then_inc(s_dve, 1)
                dve.wait_ge(s_dve, steps[0])

            def prep(k):
                c, at = CHUNKS[k], slice(COL0[k], COL0[k + 1])
                e = slice(0, EP)
                if k == 0:
                    dve.wait_ge(s_rows, 16)
                link(dve.tensor_scalar(t0[e, 0:c], rows[e, at], 8, None, ALU.arith_shift_right))
                dve.tensor_copy(binb[e, 0:c], t0[e, 0:c])
                link(dve.tensor_scalar(t1[e, 0:c], rows[e, at], R - 1, None, ALU.bitwise_and))
                if k == 0:
                    dve.wait_ge(s_cols, 16)
                link(dve.scalar_tensor_tensor(out=pk[e, 0:c], in0=t1[e, 0:c], scalar=float(1 << COLBITS),
                                              in1=cols[e, at], op0=ALU.mult, op1=ALU.add))
                link(dve.tensor_scalar(t0[e, 0:c], pk[e, 0:c], (1 << LO) - 1, None, ALU.bitwise_and))
                link(dve.tensor_scalar(t1[e, 0:c], pk[e, 0:c], LO, None, ALU.arith_shift_right))
                dve.tensor_scalar(lo[e, 0:c], t0[e, 0:c], 1.0 / 64, None, ALU.mult)
                dve.tensor_scalar(hi[e, 0:c], t1[e, 0:c], float(1 << LO) / 64, None, ALU.mult)
                if k == 0:
                    dve.wait_ge(s_vals, 16)
                link(dve.tensor_copy(vb[e, 0:c], vals[e, at]))
                dve.tensor_copy(v1[e, 0:c], vb[e, 0:c])
                link(dve.tensor_tensor(r1[e, 0:c], vals[e, at], vb[e, 0:c], ALU.subtract))
                link(dve.tensor_copy(vb[e, 0:c], r1[e, 0:c]))
                dve.tensor_copy(v2[e, 0:c], vb[e, 0:c])
                link(dve.tensor_tensor(v3[e, 0:c], r1[e, 0:c], vb[e, 0:c], ALU.subtract))

            def rank(k):
                c, e = CHUNKS[k], slice(0, EP)
                oh2, seen2 = (v[e, 0:NB * c].rearrange("p (b c) -> p b c", c=c) for v in (oh, seen))

                def onehot(i):
                    for u in range(BG):
                        dve.tensor_scalar(oh2[:, bass.ds(i * BG + u, 1), :].rearrange("p a c -> p (a c)"),
                                          binb[e, 0:c], iota_r[e, bass.ds(i * BG + u, 1)], None,
                                          ALU.is_equal).then_inc(s_oh, 1)
                loop(dve, NB // BG, onehot)
                dve.wait_ge(s_oh, (k + 1) * NB)
                link(dve.tensor_tensor_scan(seen[e, 0:NB * c], ones_f[e, 0:1].to_broadcast([EP, NB * c]),
                                            oh[e, 0:NB * c], 0.0, ALU.mult, ALU.add))
                link(dve.tensor_copy(upto[e, :].unsqueeze(2), seen2[:, :, c - 1:c]))
                dve.tensor_copy(hist[e, 0:1], upto[e, 0:1])
                link(dve.tensor_tensor(hist[e, 1:NB], upto[e, 1:NB], upto[e, 0:NB - 1], ALU.subtract))
                dve.sem_inc(s_hist, 1)
                link(dve.tensor_tensor(upto[e, :], hist[e, :], upto[e, :], ALU.subtract))
                dve.wait_ge(s_cum, k + 1)
                link(dve.tensor_scalar(tiles_i[:], ps_rank[1][:, 0:NB], float(P - 1), None, ALU.add))
                link(dve.tensor_scalar(tiles_i[:], tiles_i[:], 7, None, ALU.arith_shift_right))
                link(dve.tensor_copy(tiles_f[:], tiles_i[:]))
                link(dve.tensor_tensor_scan(tiles_inc[:], ones_f[:, 0:NB], tiles_f[:], 0.0, ALU.mult, ALU.add))
                link(dve.tensor_tensor(base[:], tiles_inc[:], tiles_f[:], ALU.subtract))
                link(dve.tensor_scalar(base[:], base[:], float(P), -1.0, ALU.mult, ALU.add))
                link(dve.tensor_tensor(base[e, :], base[e, :], ps_rank[1][e, NB:2 * NB], ALU.add))
                link(dve.tensor_tensor(base[e, :], base[e, :], upto[e, :], ALU.add))
                link(dve.tensor_tensor(past[:], iota_tq[:].unsqueeze(2).to_broadcast([P, QT, NB - 1]),
                                       tiles_inc[:, 0:NB - 1].unsqueeze(1).to_broadcast([P, QT, NB - 1]),
                                       ALU.is_ge))
                link(dve.tensor_reduce(bin_of[:], past[:], AX.X, ALU.add))
                dve.tensor_scalar(bin_of[:], bin_of[:], float(R), None, ALU.mult).then_inc(s_binof, 1)

                def pick(i):
                    for u in range(BG):
                        dve.wait_ge(s_pickf, k * NB + i * BG + u + 1)
                        b = bass.ds(i * BG + u, 1)
                        dve.scalar_tensor_tensor(out=picked[e, u, 0:c],
                                                 in0=seen2[:, b, :].rearrange("p a c -> p (a c)"), scalar=base[e, b],
                                                 in1=oh2[:, b, :].rearrange("p a c -> p (a c)"),
                                                 op0=ALU.add, op1=ALU.mult).then_inc(s_pick, 1)
                loop(dve, NB // BG, pick)
                dve.wait_ge(s_row1, k + 1)
                dve.tensor_copy(tab[0:1, TILE0[k]:TILE0[k + 1]], ps_rank[1][0:1, 0:CAPS[k]])
                dve.wait_ge(s_rank, k + 1)
                link(dve.tensor_copy(pk[e, 0:c], ps_rank[0][e, 0:c]))
                link(dve.tensor_scalar(t0[e, 0:c], pk[e, 0:c], 7, None, ALU.arith_shift_right))
                link(dve.tensor_scalar(t1[e, 0:c], pk[e, 0:c], P - 1, None, ALU.bitwise_and))
                dve.tensor_scalar(tf[e, 0:c], t0[e, 0:c], float(-MID), None, ALU.add)
                link(dve.tensor_copy(qf[e, 0:c], t1[e, 0:c]))

            def make_unit(at0, n, k, made):
                e, cap, at = slice(0, EP), CAPS[k], bass.ds(at0, PW)

                def each(v):
                    return v[e, at].unsqueeze(2).to_broadcast([EP, PW, P])
                dve.tensor_tensor(ohq[e, n], iota_q[e, :].unsqueeze(1).to_broadcast([EP, PW, P]), each(qf),
                                  ALU.is_equal).then_inc(s_q, 1)
                for u in range(PW):
                    dve.tensor_scalar(oht[e, n, u, 0:cap], iota_t[e, 0:cap], tf[e, bass.ds(at0 + u, 1)], None,
                                      ALU.is_equal)
                dve.wait_ge(s_q, made)
                dve.tensor_tensor(ohi[e, n, :, 0:P], ohq[e, n], each(lo), ALU.mult).then_inc(s_pd, 1)

            def start_perm(k):
                for n in range(AHEAD):
                    make_unit(n * PW, n, k, made_base[k] + n + 1)

            def perm_turn(k, i, h):
                dve.wait_ge(s_pm, unit_base[k] + i * PR + h + 1)
                make_unit(i * PTURN + (h + AHEAD) * PW, (h + AHEAD) % PR, k,
                          made_base[k] + AHEAD + i * PR + h + 1)

            def evacuate(k):
                cap, at = CAPS[k], slice(TILE0[k], TILE0[k + 1])
                dve.wait_ge(s_pz, k + 1)
                dve.wait_ge(s_pd, made_base[k + 1])
                word = arena[:, word_at:word_at + cap].bitcast(I32)
                part = arena[:, part_at:part_at + cap].bitcast(I32)
                link(dve.tensor_scalar(word, ps_idx[:, 0:cap], 64.0, None, ALU.mult))
                link(dve.tensor_scalar(idx_s[:, at], word, (1 << COLBITS) - 1, None, ALU.bitwise_and))
                link(dve.tensor_scalar(part, word, COLBITS, None, ALU.arith_shift_right))
                link(dve.tensor_copy(row_s[:, at], part))
                link(dve.tensor_copy(val_s[:, at], ps_val[:, 0:cap]))
                dve.sem_inc(s_ev, 1)

            def fill(t, h):
                dve.tensor_copy(iring[:, h * W:(h + 2) * W], idx_s[:, bass.ds(t, 2 * W)]).then_inc(s_idx, 2)

            def make_hot(t, n, u):
                at = bass.ds(t, 1)
                return dve.tensor_scalar(hot[:, n, u, :], iota_r[:], row_s[:, at], val_s[:, at],
                                         ALU.is_equal, ALU.mult)

            def start_apply(k):
                first = TILE0[k] if k < K else 0
                if k:
                    dve.wait_ge(s_idx, idx_base[k])
                    dve.wait_ge(s_hot, hot_base[k])
                for h in range(0, RING, 2):
                    fill(first + h * W, h)
                for n in range(2):
                    for u in range(W):
                        ins = make_hot(first + n * W + u, n, u)
                    ins.then_inc(s_hot, 1)

            regs = [[dve.alloc_register(f"bin_{h}_{u}") for u in range(W)] for h in range(2)]

            def apply_turn(k, i, h):
                n = h % 2
                first = TILE0[k] if k < K else 0
                t = i * ROUND + (first + h * W)
                done = mm_base[k] * W
                dve.load(regs[h % 2], tab[0:1, bass.ds(t, W)])
                offs = [dve.snap(r, min_val=0, max_val=(NB - 1) * R) for r in regs[h % 2]]
                dve.wait_ge(s_mm, mm_base[k] + i * RING + h + 1)
                if n:
                    fill(t + (ROUND - W), h - 1)
                for u in range(W):
                    part = target(k)[:, bass.ds(offs[u], R)]
                    dve.wait_ge(s_acc, 1 + done + i * ROUND + h * W + u)
                    ins = dve.tensor_tensor(part, part, ps_app[n][:, u, :], ALU.add)
                    ins.then_inc(s_acc, 1)
                    last = make_hot(t + 2 * W + u, n, u)
                last.then_inc(s_hot, 1)
                dve.wait_ge(s_acc, 1 + done + i * ROUND + h * W + W)
                dve.sem_inc(s_add, 1)

            def target(k):
                return acc if k < K else total

            dve.sem_inc(s_acc, 1)
            dve.sem_inc(s_add, 2)
            dve.wait_ge(s_const, CONSTS)
            prep(0)
            rank(0)
            start_perm(0)
            loop(dve, CHUNKS[0] // PTURN, lambda i: [perm_turn(0, i, h) for h in range(PR)])
            dve.wait_ge(s_clear, CLEARED)
            evacuate(0)
            for k in range(K):
                start_apply(k)
                if k + 1 < K:
                    prep(k + 1)
                    rank(k + 1)
                    start_perm(k + 1)
                else:
                    link(dve.memset(total[:, FULL * D:NBLK * D], 0.0))
                    dve.sem_inc(s_sorted, 1)
                merged(dve, k, apply_turn, perm_turn)
                if k + 1 < K:
                    evacuate(k + 1)
            dve.sem_inc(s_h1, 1)
            dve.wait_ge(s_emb, 16 * (PIECES + 1))
            dve.tensor_tensor(total, total, acc, ALU.add).then_inc(s_total, 1)
            dve.wait_ge(s_ids, 48)
            link(dve.tensor_copy(items_f, items_i))
            link(dve.tensor_scalar(wrap, items_f, 0.0, float(N), ALU.is_lt, ALU.mult))
            link(dve.tensor_tensor(items_f, items_f, wrap, ALU.add))
            link(dve.tensor_scalar(items_f, items_f, 0.0, float(N - 1), ALU.max, ALU.min))
            link(dve.tensor_copy(alias_f, alias_i))
            link(dve.tensor_scalar(mask, inputs_i, 0.0, None, ALU.not_equal))
            link(dve.tensor_reduce(n_in[:], mask, AX.X, ALU.add))
            link(dve.reciprocal(cinv[:], n_in[:]))
            link(dve.memset(idx_f, 0.0))
            dve.wait_ge(s_total, 1)
            dve.sem_inc(s_sel, 1)
            start_apply(K)

            def select(i):
                dve.wait_ge(s_sel, ST * i + 1)
                for t in range(ST):
                    dve.scalar_tensor_tensor(out=scrap[:, t, :], in0=iota_r[:, 0:L], scalar=alias_f[:, t, bass.ds(i, 1)],
                                             in1=items_f[:, t, :], op0=ALU.is_equal, op1=ALU.mult,
                                             accum_out=idx_f[:, t, bass.ds(i, 1)]).then_inc(s_sel, 1)
            loop(dve, L, lambda i: [select(i), [apply_turn(K, i, h) for h in range(RING)]])
            loop(dve, phases[K] // RING, lambda i: [apply_turn(K, i, h) for h in range(RING)], L)

            dve.wait_ge(s_sel, 1 + ST * L)
            dve.wait_ge(s_hot, hot_base[K + 1])
            dve.sem_inc(s_l2, 1)
            dve.wait_ge(s_feat, 16 * (PIECES + 1))
            w = NBLK // PIECES * D
            for q in range(PIECES):
                at = slice(q * w, q * w + w)
                dve.scalar_tensor_tensor(out=acc[:, at], in0=total[:, at], scalar=1.0 / 3, in1=acc[:, at],
                                         op0=ALU.mult, op1=ALU.add).then_inc(s_comb, 1)

            def fill_session(t, par):
                dve.tensor_copy(idx50[:, par, :], idx_f[:, t, :] if isinstance(t, int) else
                                idx_f[:, bass.ds(t, 1), :].rearrange("p a l -> p (a l)")).then_inc(s_sidx, 1)
            fill_session(0, 0)
            total3 = total.rearrange("p (b d) -> p b d", d=D)
            dve.sem_inc(s_rss[1], RB)

            def squares(i):
                dve.wait_ge(s_rss[1], RB * i + RB)
                for u in range(RB):
                    b = bass.ds(i * RB + (RA + u), 1)
                    row = total3[:, b, :].rearrange("p a d -> p (a d)")
                    dve.scalar_tensor_tensor(out=square[:, 1, u, :], in0=row, scalar=1.0, in1=row, op0=ALU.mult,
                                             op1=ALU.mult, accum_out=row_ss[:, b]).then_inc(s_rss[1], 1)
            loop(dve, (NBLK - RA) // RB, squares)
            dve.wait_ge(s_combw, 16 * PIECES)
            fill_session(1, 1)
            dve.sem_inc(s_used, 2 * (L // GL))
            dve.wait_ge(s_rroot, 1)
            link(dve.tensor_scalar(row_n[:], row_n[:], 1.0 / 3, EPS, ALU.mult, ALU.max))
            link(dve.reciprocal(row_n[:], row_n[:]))
            link(dve.tensor_scalar(row_n[:], row_n[:], 1.0 / 3, None, ALU.mult))

            def scale_rows(first, count, n, r):
                wait(dve, s_turned, r - 1)
                dve.tensor_tensor(turn_in[:, n, 0:count, :], total3[:, bass.ds(first, count), :],
                                  row_n[:, bass.ds(first, count)].unsqueeze(2).to_broadcast([P, count, D]),
                                  ALU.mult).then_inc(s_scaled, 1)
            scale_rows(0, SG, 0, 0)
            scale_rows(SG, SG, 1, 1)

            def scale_two(i):
                for n in range(2):
                    scale_rows(i * 2 * SG + n * SG, SG, n, 2 * i + n)
            loop(dve, TR // 2, scale_two, 1)
            scale_rows(TR * SG, NBLK - TR * SG, 0, TR)

            def add_places(sums, rows, weights, g, s, before, read, reads):
                l0, wl = SGS[g]
                if g == 0:
                    wait(dve, read, reads)
                else:
                    dve.wait_ge(s, before + g)
                for u in range(wl):
                    if g == 0:
                        ins = dve.tensor_scalar(sums[:, u, :], rows[:, u, :], weights(u), None, ALU.mult)
                    else:
                        ins = dve.scalar_tensor_tensor(out=sums[:, u, :], in0=rows[:, l0 + u, :],
                                                       scalar=weights(l0 + u), in1=sums[:, u, :],
                                                       op0=ALU.mult, op1=ALU.add)
                ins.then_inc(s, 1)

            def join(sums, s, before):
                dve.wait_ge(s, before + NG)
                h = SG // 2
                dve.tensor_tensor(sums[:, 0:h, :], sums[:, 0:h, :], sums[:, h:SG, :], ALU.add).then_inc(s_join, 1)

            def step(t, par, gated, c):
                first = not (isinstance(t, int) and t >= ST)

                def gather_side(g):
                    dve.wait_ge(s_tr, t * NG + g + 1)
                    add_places(hs, seq[par], lambda l: mask[:, bass.ds(t, 1), l], g, s_hsl, t * NG,
                               s_hsn, t)

                def gate_side(g):
                    l0, wl = SGS[g]
                    dve.wait_ge(s_bt, (t - 1) * NG + g + 1)
                    at = slice(l0, l0 + wl)
                    dve.tensor_tensor(beta[:, at], ps_beta[g % 2][:, at],
                                      mask[:, bass.ds(t - 1, 1), at].rearrange("p a l -> p (a l)"),
                                      ALU.mult).then_inc(s_beta, 1)
                    dve.wait_ge(s_beta, (t - 1) * NG + g + 1)
                    add_places(sess, seq[1 - par], lambda l: beta[:, l:l + 1], g, s_sel_l, (t - 1) * NG,
                               s_sess, t - 1)
                    for q in range(L // GL):
                        if l0 < (q + 1) * GL <= l0 + wl:
                            dve.wait_ge(s_sel_l, (t - 1) * NG + g + 1)
                            dve.sem_inc(s_used, 1)

                def gate_input(g):
                    l0, wl = SGS[g]
                    if g == 0:
                        dve.wait_ge(s_hwc, t)
                    dve.wait_ge(s_z, (t - 1) * NG + g + 1)
                    wait(dve, s_bt, (t - 1) * NG + g - 1)
                    dve.tensor_tensor(gate[:, ((1 - par) * NG + g) % 2, 0:wl * P].rearrange("p (l s) -> p l s", s=P),
                                      ps_hid[0][:, 0:wl * P].rearrange("p (l s) -> p l s", s=P),
                                      hs_w.unsqueeze(1).to_broadcast([P, wl, P]), ALU.add).then_inc(s_zin, 1)
                for g in range(NG):
                    if gated and g:
                        gate_input(g - 1)
                    if c:
                        for j in score_blocks(g):
                            evacuate_scores(dve, 0, c, j)
                    if first:
                        gather_side(g)
                    if gated and g > 1:
                        gate_side(g - 2)
                if gated:
                    gate_input(NG - 1)
                if c:
                    for j in score_blocks(NG):
                        evacuate_scores(dve, 0, c, j)
                if first:
                    join(hs, s_hsl, t * NG)
                    dve.wait_ge(s_join, t + max(0, t - 1) + 1 if isinstance(t, int) else 2 * t)
                    dve.tensor_tensor(hs[:, 0, :], hs[:, 0, :], hs[:, 1, :], ALU.add).then_inc(s_hsum, 1)
                    dve.wait_ge(s_hsum, t + 1)
                    wait(dve, s_ht, t)
                    dve.tensor_scalar(hs_n, hs[:, 0, :], cinv[:, bass.ds(t, 1)], None, ALU.mult).then_inc(s_hsn, 1)
                if gated:
                    gate_side(NG - 2)
                    gate_side(NG - 1)
                    join(sess, s_sel_l, (t - 1) * NG)
                    dve.wait_ge(s_join, min(t + 1, ST) + t if isinstance(t, int) else 2 * t + 1)
                    wait(dve, s_sst, t - 1)
                    dve.tensor_tensor(sess_n, sess[:, 0, :], sess[:, 1, :], ALU.add).then_inc(s_sess, 1)
                    dve.wait_ge(s_sess, t)
                    dve.scalar_tensor_tensor(out=sess_sq, in0=sess_n, scalar=1.0, in1=sess_n, op0=ALU.mult,
                                             op1=ALU.mult, accum_out=ss[:, 1 - par:2 - par]).then_inc(s_ss, 1)
                if first and not (isinstance(t, int) and t + 2 > ST):
                    fill_session(t + 2, par)
                if gated:
                    r = rsc[:, 1 - par:2 - par]
                    dve.wait_ge(s_root, t)
                    dve.tensor_scalar(r, root[:, 1 - par:2 - par], EPS, None, ALU.max).then_inc(s_rsteps, 1)
                    dve.wait_ge(s_rsteps, 2 * t - 1)
                    dve.reciprocal(r, r).then_inc(s_rsteps, 1)
                    dve.wait_ge(s_rsteps, 2 * t)
                    dve.tensor_scalar(r, r, W_K, None, ALU.mult).then_inc(s_rsc, 1)
            dve.sem_inc(s_scev[0], 1)
            session_steps(dve, step)

        @block.tensor
        def _(pe):
            pe.wait_ge(s_const, CONSTS)
            pe.sem_inc(s_pm, PR - AHEAD)
            pe.sem_inc(s_pickf, BG)
            pe.wait_ge(s_w, 16 * 7)
            pe.transpose(ps_app[0][:, 0, 0:P], g1[:], ident[:])
            pe.transpose(ps_app[0][:, 0, P:2 * P], g2[:], ident[:])
            pe.transpose(ps_app[0][:, 1, 0:L], pos[:], ident[0:L, 0:L]).then_inc(s_wt, 1)
            pe.wait_ge(s_wtc, 3)
            pe.matmul(ps_app[0][:, 1, L:2 * L], w1a[:], pos_t[:], start=True, stop=True).then_inc(s_wt, 1)
            pe.wait_ge(s_wtc, 4)

            def rank(k):
                c, e = CHUNKS[k], slice(0, EP)
                pe.wait_ge(s_hist, k + 1)
                pe.matmul(ps_rank[1][:, 0:NB], ones_f[e, :], hist[e, :], start=True, stop=True)
                pe.matmul(ps_rank[1][:, NB:2 * NB], below[e, :], hist[e, :], start=True,
                          stop=True).then_inc(s_cum, 1)
                pe.wait_ge(s_binof, k + 1)
                for q in range(-(-CAPS[k] // P)):
                    w = min(P, CAPS[k] - q * P)
                    ins = pe.matmul(ps_rank[1][0:1, q * P:q * P + w], bin_of[:, q:q + 1], ident[:, 0:w],
                                    start=True, stop=True)
                ins.then_inc(s_row1, 1)
                dst = ps_rank[0][e, 0:c]
                pe.matmul(dst, zero_b[:, e], iota_t[:, 0:c], start=True, stop=False, skip_group_check=True)

                def add_picks(i):
                    for u in range(BG):
                        pe.wait_ge(s_pick, k * NB + i * BG + u + 1)
                        pe.matmul(dst, ident[e, e], picked[e, u, 0:c], start=False, stop=False,
                                  skip_group_check=True).then_inc(s_pickf, 1)
                loop(pe, NB // BG, add_picks)
                pe.matmul(dst, zero_b[:, e], iota_t[:, 0:c], start=False, stop=True,
                          skip_group_check=True).then_inc(s_rank, 1)

            def open_banks(k):
                if k:
                    pe.wait_ge(s_ev, k)
                for b in (ps_idx, ps_val):
                    pe.matmul(b[:, 0:CAPS[k]], zero_b[:, :], iota_t[:, 0:CAPS[k]], start=True, stop=False,
                              skip_group_check=True)

            def perm_turn(k, i, h):
                n, cap = h, CAPS[k]
                pe.wait_ge(s_pa, unit_base[k] + i * PR + h + 1)
                if k == 0:
                    pe.wait_ge(s_pp, 2 * (i * PR + h + 1))
                for u in range(PW):
                    o = oht[0:EP, n, u, 0:cap]
                    for m in range(2):
                        pe.matmul(ps_idx[:, 0:cap], ohi[0:EP, n, u, m * P:m * P + P], o,
                                  start=False, stop=False, skip_group_check=True)
                    for m in range(3):
                        ins = pe.matmul(ps_val[:, 0:cap], ohv[0:EP, n, u, m * P:m * P + P], o,
                                        start=False, stop=False, skip_group_check=True)
                ins.then_inc(s_pm, 1)

            def close_banks(k):
                for b in (ps_idx, ps_val):
                    ins = pe.matmul(b[:, 0:CAPS[k]], zero_b[:, :], iota_t[:, 0:CAPS[k]], start=False, stop=True,
                                    skip_group_check=True)
                ins.then_inc(s_pz, 1)

            def apply_turn(k, i, h):
                n = h % 2
                used = mm_base[k] // RING * 64
                pe.wait_ge(s_hot, hot_base[k] + i * RING + h + 1)
                pe.wait_ge(s_g[h], used + i * 64 + 64)
                pe.wait_ge(s_add, mm_base[k] + i * RING + h + 1)
                for u in range(W):
                    for r in range(R // P):
                        ins = pe.matmul(ps_app[n][:, u, r * P:r * P + P], hot[:, n, u, r * P:r * P + P],
                                        gath[:, h, u, :], start=True, stop=True)
                ins.then_inc(s_mm, 1)

            rank(0)
            open_banks(0)
            loop(pe, CHUNKS[0] // PTURN, lambda i: [perm_turn(0, i, h) for h in range(PR)])
            close_banks(0)
            for k in range(K):
                if k + 1 < K:
                    rank(k + 1)
                    open_banks(k + 1)
                merged(pe, k, apply_turn, perm_turn)
                if k + 1 < K:
                    close_banks(k + 1)
            loop(pe, phases[K] // RING, lambda i: [apply_turn(K, i, h) for h in range(RING)])

            def turn_rows(count, n, r):
                pe.wait_ge(s_scaled, r + 1)
                wait(pe, s_norm, r - 1)
                for b in range(count):
                    ins = pe.transpose(ps_turn[n][:, b * P:b * P + P], turn_in[:, n, b, :], ident[:])
                ins.then_inc(s_turned, 1)
            turn_rows(SG, 0, 0)
            turn_rows(SG, 1, 1)
            loop(pe, TR // 2, lambda i: [turn_rows(SG, n, 2 * i + n) for n in range(2)], 1)
            turn_rows(NBLK - TR * SG, 0, TR)
            pe.wait_ge(s_norm, TR + 1)

            def scores(c, j):
                i, par = c
                b, n, at, w = score_block(c, j)
                if j == 0:
                    pe.wait_ge(s_sstc, 2 * i + par + 1)
                pe.wait_ge(s_scev[b], n)
                pe.matmul(ps_score[b][:, 0:w], sess_t[:, par, :], total[:, at:at + w],
                          start=True, stop=True).then_inc(s_sc[b], 1)

            def step(t, par, gated, c):
                first = not (isinstance(t, int) and t >= ST)
                half = t // 2 if isinstance(t, int) else c[0] + 1

                def turn(g):
                    l0, wl = SGS[g]
                    n = (par * NG + g) % 2
                    wait(pe, s_seqt, t * NG + g - 1)
                    for l in range(l0, l0 + wl):
                        if l % GL == 0:
                            pe.wait_ge(s_seq[par][l // GL], (half + 1) * (16 * GL))
                        ins = pe.transpose(ps_turn[n][:, (l - l0) * P:(l - l0 + 1) * P], seq[par][:, l, :], ident[:])
                    ins.then_inc(s_tr, 1)

                def hidden(g):
                    l0, wl = SGS[g]
                    pe.wait_ge(s_seqt, t * NG + g + 1)
                    wait(pe, s_tanh, t * NG + g)
                    pe.matmul(ps_hid[1][:, 0:wl * P], w1b[:], seq_t[:, (par * NG + g) % 2, 0:wl * P],
                              start=True, stop=True).then_inc(s_m1, 1)

                def gate_input(g):
                    l0, wl = SGS[g]
                    pe.wait_ge(s_tanh, (t - 1) * NG + g + 1)
                    wait(pe, s_zin, (t - 1) * NG + g)
                    pe.matmul(ps_hid[0][:, 0:wl * P], g1_t[:], nh[:, l0 * P:(l0 + wl) * P], start=True,
                              stop=True).then_inc(s_z, 1)

                def weigh(g):
                    l0, wl = SGS[g]
                    pe.wait_ge(s_gate, (t - 1) * NG + g + 1)
                    if g >= 2:
                        pe.wait_ge(s_beta, (t - 1) * NG + g - 1)
                    n = ((1 - par) * NG + g) % 2
                    for l in range(l0, l0 + wl):
                        ins = pe.matmul(ps_beta[g % 2][:, l:l + 1], gate[:, n, (l - l0) * P:(l - l0 + 1) * P], w2[:],
                                        start=True, stop=True)
                    ins.then_inc(s_bt, 1)
                for g in range(NG):
                    if c:
                        for j in score_blocks(g):
                            scores(c, j)
                    if first:
                        turn(g)
                    if first and g:
                        hidden(g - 1)
                    if gated:
                        gate_input(g)
                    if c and g == 0:
                        pe.wait_ge(s_sess, t - 1)
                        pe.transpose(ps_sess, sess_n, ident[:]).then_inc(s_sst, 1)
                    if gated and g == 0:
                        pe.wait_ge(s_hsn, t)
                        pe.transpose(ps_mean, hs_n, ident[:]).then_inc(s_ht, 1)
                        pe.wait_ge(s_htc, t)
                        pe.matmul(ps_hw, g2_t[:], hs_t, start=True, stop=True).then_inc(s_hw, 1)
                    if gated and g > 1:
                        weigh(g - 2)
                if c:
                    for j in score_blocks(NG):
                        scores(c, j)
                if first:
                    hidden(NG - 1)
                if gated:
                    weigh(NG - 2)
                    weigh(NG - 1)
            session_steps(pe, step)

        @block.scalar
        def _(act):
            def perm_turn(k, i, h):
                n, e = h, slice(0, EP)
                act.wait_ge(s_pd, made_base[k] + i * PR + h + 1)
                for u in range(PW):
                    at = bass.ds(i * PTURN + h * PW + u, 1)
                    if k:
                        act.activation(ohi[e, n, u, P:2 * P], ohq[e, n, u, :], ACT.Copy, scale=hi[e, at])
                    for m, v in enumerate((v1, v2, v3)):
                        if k == 0 and m == 0:
                            continue
                        ins = act.activation(ohv[e, n, u, m * P:m * P + P], ohq[e, n, u, :], ACT.Copy,
                                             scale=v[e, at])
                ins.then_inc(s_pa, 1)

            act.wait_ge(s_wt, 1)
            act.activation(g1_t[:], ps_app[0][:, 0, 0:P], ACT.Copy).then_inc(s_wtc, 1)
            act.activation(g2_t[:], ps_app[0][:, 0, P:2 * P], ACT.Copy).then_inc(s_wtc, 1)
            act.activation(pos_t[:], ps_app[0][:, 1, 0:L], ACT.Copy).then_inc(s_wtc, 1)
            act.wait_ge(s_wt, 2)
            act.activation(pos_w[:], ps_app[0][:, 1, L:2 * L], ACT.Copy).then_inc(s_wtc, 1)
            for k in range(K):
                loop(act, CHUNKS[k] // PTURN, lambda i: [perm_turn(k, i, h) for h in range(PR)])

            act.wait_ge(s_l2, 1)
            total3 = total.rearrange("p (b d) -> p b d", d=D)
            act.sem_inc(s_rss[0], RB)

            def squares(i):
                act.wait_ge(s_rss[0], RB * i + RB)
                for u in range(RB):
                    b = bass.ds(i * RB + u, 1)
                    act.activation(square[:, 0, u, :], total3[:, b, :].rearrange("p a d -> p (a d)"), ACT.Square,
                                   accum_out=row_ss[:, b]).then_inc(s_rss[0], 1)
            loop(act, RA // RB, squares)
            act.wait_ge(s_rss[0], RB + RA)
            act.wait_ge(s_rss[1], RB + NBLK - RA)
            act.activation(row_n[:], row_ss[:], ACT.Sqrt).then_inc(s_rroot, 1)

            def place(first, count, n, r):
                act.wait_ge(s_turned, r + 1)
                act.activation(total[:, bass.ds(first * P, count * P)], ps_turn[n][:, 0:count * P],
                               ACT.Copy).then_inc(s_norm, 1)
            loop(act, TR // 2, lambda i: [place(i * 2 * SG + n * SG, SG, n, 2 * i + n) for n in range(2)])
            place(TR * SG, NBLK - TR * SG, 0, TR)

            def step(t, par, gated, c):
                first = not (isinstance(t, int) and t >= ST)

                def hidden(g):
                    l0, wl = SGS[g]
                    act.wait_ge(s_m1, t * NG + g + 1)
                    for l in range(l0, l0 + wl):
                        ins = act.activation(nh[:, l * P:l * P + P], ps_hid[1][:, (l - l0) * P:(l - l0 + 1) * P],
                                             ACT.Tanh, bias=pos_w[:, L - 1 - l:L - l])
                    ins.then_inc(s_tanh, 1)

                def copy(g):
                    l0, wl = SGS[g]
                    n = (par * NG + g) % 2
                    act.wait_ge(s_tr, t * NG + g + 1)
                    wait(act, s_m1, t * NG + g - 1)
                    act.activation(seq_t[:, n, 0:wl * P], ps_turn[n][:, 0:wl * P], ACT.Copy).then_inc(s_seqt, 1)

                def gates(g):
                    l0, wl = SGS[g]
                    act.wait_ge(s_zin, (t - 1) * NG + g + 1)
                    z = gate[:, ((1 - par) * NG + g) % 2, 0:wl * P]
                    act.activation(z, z, ACT.Sigmoid, bias=gb[:]).then_inc(s_gate, 1)
                if c:
                    act.wait_ge(s_sst, t - 1)
                    act.activation(sess_t[:, par, :], ps_sess, ACT.Copy).then_inc(s_sstc, 1)
                if gated:
                    act.wait_ge(s_ht, t)
                    act.activation(hs_t, ps_mean, ACT.Copy).then_inc(s_htc, 1)
                    act.wait_ge(s_hw, t)
                    act.activation(hs_w, ps_hw, ACT.Copy).then_inc(s_hwc, 1)
                for g in range(NG):
                    if gated and g:
                        gates(g - 1)
                    if c:
                        for j in score_blocks(g):
                            evacuate_scores(act, 1, c, j)
                    if first:
                        copy(g)
                    if first and g:
                        hidden(g - 1)
                if gated:
                    gates(NG - 1)
                if c:
                    for j in score_blocks(NG):
                        evacuate_scores(act, 1, c, j)
                if first:
                    hidden(NG - 1)
                if gated:
                    act.wait_ge(s_ss, t)
                    act.activation(root[:, 1 - par:2 - par], ss[:, 1 - par:2 - par], ACT.Sqrt).then_inc(s_root, 1)
            act.sem_inc(s_scev[1], 1)
            session_steps(act, step)


_INS = {"items": "r_items", "inputs": "r_inputs", "alias": "r_alias_inputs", "feat": "L0_rec_item_features",
        "row": "L0_rec_adj_row", "col": "L0_rec_adj_col", "val": "L0_rec_adj_val", "emb": "L0_rec_emb",
        "w1": "L0_rec_w_1", "w2": "L0_rec_w_2", "g1": "L0_rec_glu1_w", "gb": "L0_rec_glu1_b", "g2": "L0_rec_glu2_w"}


def kernel(**inputs):
    import concourse.bacc as bacc
    from concourse.bass_utils import run_bass_kernel_spmd

    nc = bacc.Bacc("TRN2", target_bir_lowering=False, num_devices=1)
    arrays, x = {}, {}
    for name, full in _INS.items():
        a = np.ascontiguousarray(inputs[full])
        arrays[f"in_{name}"] = a
        x[name] = nc.dram_tensor(f"in_{name}", a.shape, mybir.dt.from_np(a.dtype), kind="ExternalInput").ap()
    out = nc.dram_tensor("scores", (B, N), F32, kind="ExternalOutput").ap()
    build(nc, x, out)
    r = run_bass_kernel_spmd(nc, [arrays], core_ids=[0])
    return r.results[0]["scores"]
```
